# Optimizing a Trainium2 kernel written in Bass

```python
import numpy as np
import jax
import jax.numpy as jnp

def _softmax(x, axis=-1):
    return jax.nn.softmax(x, axis=axis)

def _gelu(x):
    return jax.nn.gelu(x, approximate=True)

def _silu(x):
    return jax.nn.silu(x)

def _sigmoid(x):
    return jax.nn.sigmoid(x)

def _layernorm(x, axis=-1, eps=1e-05):
    m = jnp.mean(x, axis=axis, keepdims=True)
    v = jnp.var(x, axis=axis, keepdims=True)
    return (x - m) / jnp.sqrt(v + eps)

def _scatter_add(tgt, idx, src, axis=0):
    return tgt.at[idx].add(src)

def _segment_sum(src, seg, n):
    return jax.ops.segment_sum(src, seg, n)
kernel_name = 'mk_gnn_preln_d1_gnn_r64_f679d0'

def setup_inputs(seed: int=0):
    np.random.seed(seed)
    _w = jnp.asarray

    def _rec_inputs():
        import jax
        import jax.numpy as jnp
        _gk = jax.random.key(seed)
        x = -0.0003713 + 1 * jax.random.normal(jax.random.fold_in(_gk, 1), (100000, 128), jnp.float32)
        src = jax.random.randint(jax.random.fold_in(_gk, 2), (50000,), 0, 100000, jnp.int32)
        dst = jnp.minimum((100000 * jax.random.uniform(jax.random.fold_in(_gk, 3), (50000,)) ** 2.0).astype(jnp.int32), 99999)
        _o = jnp.argsort(dst, stable=True)
        src = src[_o]
        dst = dst[_o]
        edge_attr_16 = -5.3897e-05 + 0.999841 * jax.random.normal(jax.random.fold_in(_gk, 12), (50000, 16), jnp.float32)
        edge_type_2 = jax.random.randint(jax.random.fold_in(_gk, 13), (50000,), 0, 2, jnp.int32)
        return (x, src, dst, edge_attr_16, edge_type_2)
    x, src, dst, edge_attr_16, edge_type_2 = _rec_inputs()

    def _L0_gnn_setup():
        import jax, jax.numpy as jnp
        import numpy as np
        N = 100000
        E = 25000
        IN_DIM = 128
        EDGE_DIM = 16
        HID = 128
        MSG_IN = IN_DIM + EDGE_DIM + 2
        LN_EPS = 1e-05

        def _layernorm(x, gamma, beta):
            mu = jnp.mean(x, axis=-1, keepdims=True)
            var = jnp.mean(jnp.square(x - mu), axis=-1, keepdims=True)
            return (x - mu) * jax.lax.rsqrt(var + LN_EPS) * gamma + beta
        key = jax.random.key(seed)
        ks = jax.random.split(key, 16)
        s = 1.0 / np.sqrt(MSG_IN)
        s2 = 1.0 / np.sqrt(HID)
        s3 = 1.0 / np.sqrt(IN_DIM)
        return {'h': jax.random.normal(ks[0], (N, IN_DIM), dtype=jnp.float32), 'e_feat': jax.random.normal(ks[1], (E, EDGE_DIM), dtype=jnp.float32), 'src': jax.random.randint(ks[2], (E,), 0, N, dtype=jnp.int32), 'dst': jax.random.randint(ks[3], (E,), 0, N, dtype=jnp.int32), 'e_type': jax.random.randint(ks[4], (E,), 0, 2, dtype=jnp.int32), 'W1': jax.random.uniform(ks[5], (MSG_IN, HID), jnp.float32, -s, s), 'b1': jax.random.uniform(ks[6], (HID,), jnp.float32, -s, s), 'W2': jax.random.uniform(ks[7], (HID, HID), jnp.float32, -s2, s2), 'b2': jax.random.uniform(ks[8], (HID,), jnp.float32, -s2, s2), 'Ws': jax.random.uniform(ks[9], (IN_DIM, HID), jnp.float32, -s3, s3), 'bs': jax.random.uniform(ks[10], (HID,), jnp.float32, -s3, s3), 'gamma': jnp.ones((HID,), jnp.float32), 'beta': jnp.zeros((HID,), jnp.float32)}
    _L0_gnn_all = _L0_gnn_setup()
    _L0_gnn_in = {k: v for k, v in _L0_gnn_all.items() if k in ('W1', 'b1', 'W2', 'b2', 'Ws', 'bs', 'gamma', 'beta')}
    del _L0_gnn_all
    return {'x': x, 'src': src, 'dst': dst, 'edge_attr_16': edge_attr_16, 'edge_type_2': edge_type_2, 'L0_gnn_W1': _L0_gnn_in['W1'], 'L0_gnn_b1': _L0_gnn_in['b1'], 'L0_gnn_W2': _L0_gnn_in['W2'], 'L0_gnn_b2': _L0_gnn_in['b2'], 'L0_gnn_Ws': _L0_gnn_in['Ws'], 'L0_gnn_bs': _L0_gnn_in['bs'], 'L0_gnn_gamma': _L0_gnn_in['gamma'], 'L0_gnn_beta': _L0_gnn_in['beta']}

def reference(x, src, dst, edge_attr_16, edge_type_2, L0_gnn_W1, L0_gnn_b1, L0_gnn_W2, L0_gnn_b2, L0_gnn_Ws, L0_gnn_bs, L0_gnn_gamma, L0_gnn_beta):
    import jax
    import jax.numpy as jnp

    def _L0_gnn_ref(h, e_feat, src, dst, e_type, W1, b1, W2, b2, Ws, bs, gamma, beta):
        import jax, jax.numpy as jnp
        import numpy as np
        N = 100000
        E = 25000
        IN_DIM = 128
        EDGE_DIM = 16
        HID = 128
        MSG_IN = IN_DIM + EDGE_DIM + 2
        LN_EPS = 1e-05

        def _layernorm(x, gamma, beta):
            mu = jnp.mean(x, axis=-1, keepdims=True)
            var = jnp.mean(jnp.square(x - mu), axis=-1, keepdims=True)
            return (x - mu) * jax.lax.rsqrt(var + LN_EPS) * gamma + beta
        onehot = jax.nn.one_hot(e_type, 2, dtype=jnp.float32)
        z = jnp.concatenate([h[src], e_feat, onehot], axis=-1)
        m = jax.nn.relu(z @ W1 + b1) @ W2 + b2
        m_sum = jax.ops.segment_sum(m, dst, num_segments=N)
        out = h @ Ws + bs + m_sum
        out = jax.nn.relu(out)
        return _layernorm(out, gamma, beta)
    h = jnp.maximum(_layernorm(x, axis=-1), 0.0)
    x = x + _L0_gnn_ref(h, edge_attr_16, src, dst, edge_type_2, L0_gnn_W1, L0_gnn_b1, L0_gnn_W2, L0_gnn_b2, L0_gnn_Ws, L0_gnn_bs, L0_gnn_gamma, L0_gnn_beta)
    return x

_drawn_inputs = setup_inputs


def setup_inputs(seed=0):
    import zlib

    import numpy as np

    out = dict(_drawn_inputs(seed))
    spreads = {'L0_gnn_gamma': (1.0, 0.2), 'L0_gnn_beta': (0.0, 0.1)}
    factors = {}
    for name, (base, spread) in spreads.items():
        noise = np.random.default_rng([zlib.crc32(name.encode()), seed]).standard_normal(out[name].shape)
        drawn = base * np.exp(spread * noise) if base else spread * noise
        out[name] = jnp.asarray(drawn.astype(out[name].dtype))
    for name, factor in factors.items():
        out[name] = (out[name] * factor).astype(out[name].dtype)
    return out
```

```python
from contextlib import ExitStack

import numpy as np

import concourse.bass as bass
from concourse import mybir

P = 128
D = 128
N = 100000
E = 50000
EF = 16
TYPES = 2
G = 4
BLK = G * P
EB = -(-E // BLK)
ET = EB * G
EP = EB * BLK
NB = -(-N // BLK)
NP = NB * BLK
PAIR = 2 * P
PAIRS = NP // PAIR
ROW = D + 4
DST = D
QL = 32
QH = -(-PAIRS // QL)
PAIR_BITS, QL_BITS = 8, 5
EPS = 1e-5
U = 8
R = 4
PEEL = 1

C_ID = 0
C_SLOT = C_ID + P
C_BASE = C_SLOT + PAIR
C_QL = C_BASE + PAIRS
C_TRI = C_QL + QL
C_ROWS = C_TRI + P
C_TYPE = C_ROWS + P
C_EPS = C_TYPE + 1
C_END = C_EPS + 1

assert 1 << PAIR_BITS == PAIR and 1 << QL_BITS == QL and QH <= P


class Step:

    def __init__(self, turn, slot):
        self.turn, self.slot = turn, slot

    @property
    def n(self):
        return self.turn * U + self.slot

    def back(self, k):
        return Step(self.turn + (self.slot - k) // U, (self.slot - k) % U)

    def use(self, ring):
        return self.turn * (U // ring) + self.slot // ring

    def exists(self, total):
        return not isinstance(self.turn, int) or 0 <= self.n < total


def run_blocks(eng, total, lag, step):
    turns = total // U
    for n in range(PEEL * U):
        step(Step(n // U, n % U))
    with eng.Fori(PEEL, turns) as turn:
        for slot in range(U):
            step(Step(turn, slot))
    for n in range(turns * U, total + lag):
        step(Step(n // U, n % U))


def build(nc, x, src, dst, dst_next, type_rows, ef_rows, w1, b1, w2, b2, ws, bs, gamma, beta, consts, out):
    f32, bf16, i32 = mybir.dt.float32, mybir.dt.bfloat16, mybir.dt.int32
    ALU, ACT = mybir.AluOpType, mybir.ActivationFunctionType
    AX = mybir.AxisListType

    messages = nc.dram_tensor("messages", (EP + 2 * P, ROW), f32, kind="Internal").ap()
    msg_store = messages[0:EP, :].rearrange("(p b g) r -> b p g r", p=P, g=G)
    x_rows = x.rearrange("(b q p k) d -> b p q (k d)", q=2, p=P, k=2)
    out_rows = out.rearrange("(b q p k) d -> b p q (k d)", q=2, p=P, k=2)

    ctx = ExitStack()
    with ctx:
        def sb(name, shape, dt=f32):
            return ctx.enter_context(nc.sbuf_tensor(name, shape, dt))

        def pb(name, shape, dt=f32):
            return ctx.enter_context(nc.psum_tensor(name, shape, dt))

        def sem(name):
            return ctx.enter_context(nc.semaphore(name))

        cst = sb("cst", [P, C_END])
        ident = cst[:, C_ID:C_ID + P]
        slot_of = cst[:, C_SLOT:C_SLOT + PAIR]
        tri = cst[:, C_TRI:C_TRI + P]
        w1_x = sb("w1_x", [D, D])
        w1_e = sb("w1_e", [TYPES + EF, D])
        w2_sb = sb("w2_sb", [D, D])
        ws_sb = sb("ws_sb", [D, D])
        b1_col = sb("b1_col", [D, 1])
        b2_bc = sb("b2_bc", [P, D])
        bs_bc = sb("bs_bc", [P, BLK])
        gamma_bc = sb("gamma_bc", [P, D])
        beta_bc = sb("beta_bc", [P, D])
        pick_rows = sb("pick_rows", [P, P], bf16)
        bs_parts = sb("bs_parts", [P, BLK], bf16)
        bs_hi = sb("bs_hi", [P, BLK], bf16)
        bs_rest = sb("bs_rest", [P, BLK])
        src_sb = sb("src_sb", [P, ET], i32)
        dst_sb = sb("dst_sb", [P, ET], i32)
        next_sb = sb("next_sb", [P, ET], i32)
        dst_f = sb("dst_f", [P, ET])
        next_f = sb("next_f", [P, ET])
        q_int = sb("q_int", [P, 2, ET], i32)
        q_f = sb("q_f", [P, 2, ET])
        hot_h = sb("hot_h", [P, ET, QH], bf16)
        hot_l = sb("hot_l", [P, ET, QL], bf16)
        falls = sb("falls", [P, 2])
        ones = sb("ones", [P, P])
        count = sb("count", [QH, QL])
        upto = sb("upto", [QH, QL])
        total = sb("total", [QH, 2])
        offset = sb("offset", [QH, 2])
        is_sorted = sb("is_sorted", [QH, 2])
        tab_f = sb("tab_f", [QH, QL, 2])
        tab_i = sb("tab_i", [QH, QL, 2], i32)
        table = sb("table", [1, QH * QL * 2], i32)
        pad_rows = sb("pad_rows", [P, 2, ROW])
        xg = sb("xg", [P, U, G, D])
        idx = sb("idx", [P, U, G], i32)
        ty = sb("ty", [TYPES, R, BLK], i32)
        ez = sb("ez", [TYPES + EF, R, BLK])
        msg = sb("msg", [P, R, G, ROW])
        stats = sb("stats", [P, 2, G, 6])
        moments = sb("moments", [P, R, G, 2])
        std = sb("std", [P, R, G])
        rstd = sb("rstd", [P, 2, G])
        xn = sb("xn", [P, 2, G, D])
        hT = sb("hT", [D, 2, BLK])
        tT = sb("tT", [D, 2, BLK])
        xb = sb("xb", [P, U, G, D])
        win = sb("win", [P, R, 2, ROW])
        sel = sb("sel", [P, 2, 2, PAIR])
        win_x = sb("win_x", [P, 4, 2, ROW])
        sel_x = sb("sel_x", [P, 4, 2, PAIR])
        r = sb("r", [P, R, G, D])
        stats2 = sb("stats2", [P, 2, G, 6])
        moments2 = sb("moments2", [P, R, G, 2])
        std2 = sb("std2", [P, R, G])
        rstd2 = sb("rstd2", [P, 2, G])
        y = sb("y", [P, R, G, D])

        ps_t = [pb(f"ps_t{i}", [D, BLK]) for i in range(2)]
        ps_z = [pb(f"ps_z{i}", [D, BLK]) for i in range(2)]
        ps_m = [pb(f"ps_m{i}", [P, BLK]) for i in range(2)]
        ps_q = pb("ps_q", [QH, BLK])

        s_idx = sem("src_loaded")
        s_lists = sem("dst_loaded")
        s_cst = sem("consts_loaded")
        s_w = sem("weights_loaded")
        s_gather = [sem(f"gathered{i}") for i in range(U)]
        s_ez = [sem(f"edge_feats_loaded{i}") for i in range(R)]
        s_ty = [sem(f"types_loaded{i}") for i in range(R)]
        s_mst = [sem(f"messages_stored{i}") for i in range(R)]
        s_pad = sem("pad_rows_stored")
        s_tab = sem("table_ready")
        s_x = [sem(f"x_loaded{i}") for i in range(U)]
        s_win = [sem(f"windows_loaded{i}") for i in range(R)]
        s_winx = [sem(f"extra_windows_loaded{i}") for i in range(4)]
        s_out = [sem(f"out_stored{i}") for i in range(R)]
        s_set = sem("setup_chain")
        s_passed = sem("waits_passed")
        s_fill = sem("fills_done")
        s_bias = sem("bias_parts_ready")
        s_hot = sem("one_hots_ready")
        s_hist = sem("histogram_ready")
        s_tot = sem("totals_ready")
        s_off = sem("offsets_ready")
        s_tabi = sem("table_computed")
        e_idx = sem("edge_indices")
        e_stats = sem("edge_stats")
        e_mom = sem("edge_moments")
        e_std = sem("edge_std")
        e_rstd = sem("edge_rstd")
        e_norm = sem("edge_normed")
        e_type = sem("edge_types_hot")
        e_tr = sem("edge_transposed")
        e_h = sem("edge_hT")
        e_z = sem("edge_z")
        e_t = sem("edge_tT")
        e_m = sem("edge_m")
        e_msg = sem("edge_msg")
        n_stats = sem("node_stats")
        n_mom = sem("node_moments")
        n_std = sem("node_std")
        n_rstd = sem("node_rstd")
        n_norm = sem("node_normed")
        n_tr = sem("node_transposed")
        n_h = sem("node_hT")
        n_sel = sem("node_sel")
        n_xb = sem("node_x_beta")
        n_u = sem("node_u")
        n_r = sem("node_r")
        n_stats2 = sem("node_stats2")
        n_mom2 = sem("node_moments2")
        n_std2 = sem("node_std2")
        n_rstd2 = sem("node_rstd2")
        n_cen = sem("node_centred")
        n_y = sem("node_y")
        x_sel = [sem(f"extra_sel{i}") for i in range(4)]
        x_used = [sem(f"extra_used{i}") for i in range(4)]

        def extra_slot(s, q):
            return 2 * (s.slot % 2) + q

        def wait_ahead(eng, semaphore, value):
            eng.wait_ge(semaphore, value)
            eng.sem_inc(s_passed, 1)

        def load_table(eng, s):
            row = table[0:1, bass.ds(s.n * 4, 4)]
            _, v = nc.values_load_multi_w_load_instructions(
                row, engines=[eng.engine], min_val=0, max_val=EP,
                skip_runtime_bounds_check_because="the table's entries are at most EP by its construction")
            return v

        block = ctx.enter_context(nc.Block())

        @block.sync
        def _(sp):
            sp.dma_start(src_sb[:, :], src).then_inc(s_idx, 16)
            sp.dma_start(dst_sb[:, :], dst).then_inc(s_lists, 16)
            sp.dma_start(next_sb[:, :], dst_next).then_inc(s_lists, 16)
            sp.dma_start(cst[:, :], consts).then_inc(s_cst, 16)
            sp.dma_start(w1_x[:, :], w1[0:D, :]).then_inc(s_w, 16)
            sp.dma_start(w1_e[0:TYPES, :], w1[D + EF:D + EF + TYPES, :]).then_inc(s_w, 16)
            sp.dma_start(w1_e[TYPES:TYPES + EF, :], w1[D:D + EF, :]).then_inc(s_w, 16)
            sp.dma_start(w2_sb[:, :], w2).then_inc(s_w, 16)
            sp.dma_start(b1_col[:, :], b1).then_inc(s_w, 16)
            sp.dma_start(b2_bc[:, :], b2.partition_broadcast(P)).then_inc(s_w, 16)
            sp.dma_start(ws_sb[:, :], ws).then_inc(s_w, 16)
            sp.dma_start(bs_bc[:, :], bs.partition_broadcast(P)).then_inc(s_w, 16)
            sp.dma_start(gamma_bc[:, :], gamma.partition_broadcast(P)).then_inc(s_w, 16)
            sp.dma_start(beta_bc[:, :], beta.partition_broadcast(P)).then_inc(s_w, 16)

            def edge_step(s):
                if s.exists(EB):
                    if s.back(R).exists(EB):
                        sp.wait_ge(e_z, s.back(R).n + 1)
                    sp.dma_start(ty[:, s.slot % R, :], type_rows[bass.ds(s.n, 1), :, :].rearrange("a t e -> (a t) e"))\
                      .then_inc(s_ty[s.slot % R], 16)
                    sp.dma_start(ez[TYPES:, s.slot % R, :], ef_rows[bass.ds(s.n, 1), :, :].rearrange("a t e -> (a t) e"))\
                      .then_inc(s_ez[s.slot % R], 16)
                m = s.back(3)
                if m.exists(EB):
                    sp.wait_ge(e_msg, m.n + 1)
                    sp.dma_start(msg_store[bass.ds(m.n, 1), :, :, :].rearrange("a p g r -> (a p) g r"),
                                 msg[:, m.slot % R, :, :]).then_inc(s_mst[m.slot % R], 16)

            run_blocks(sp, EB, 3, edge_step)
            sp.wait_ge(s_fill, 1)
            sp.dma_start(messages[EP:EP + 2 * P, :].rearrange("(p k) r -> p k r", k=2), pad_rows[:, :, :])\
              .then_inc(s_pad, 16)
            sp.wait_ge(s_tabi, 1)
            sp.dma_start(table[:, :].rearrange("o (a b) -> o a b", a=QH), tab_i[:, :, :].rearrange("a b c -> a (b c)"))\
              .then_inc(s_tab, 16)
            sp.wait_ge(s_tab, 16)
            sp.wait_ge(s_pad, 16)
            for i in range(R):
                sp.wait_ge(s_mst[i], 16 * len(range(i, EB, R)))

            doubles = [sp.alloc_register(f"sp_doubles{i}") for i in range(4)]
            for reg in doubles:
                sp.reg_mov(reg, 0)

            def node_step(s):
                if s.exists(NB):
                    free = s.back(U)
                    if free.exists(NB):
                        sp.wait_ge(n_y, free.n + 1)
                    sp.dma_start(xb[:, s.slot, :, :].rearrange("p (q k) d -> p q (k d)", q=2),
                                 x_rows[bass.ds(s.n, 1), :, :, :].rearrange("a p q f -> (a p) q f")).then_inc(s_x[s.slot], 16)
                    v = load_table(sp, s)
                    if s.back(R).exists(NB):
                        sp.wait_ge(n_u, s.back(R).n + 1)
                    for q in range(2):
                        sp.dma_start(win[:, s.slot % R, q, :], messages[bass.ds(v[2 * q], P), :])\
                          .then_inc(s_win[s.slot % R], 16)
                e = s.back(3)
                if e.exists(NB):
                    v = load_table(sp, e)
                    for q in range(2):
                        es = extra_slot(e, q)
                        with sp.If(v[2 * q + 1] > 0):
                            with sp.Fori(0, v[2 * q + 1]) as c:
                                sp.wait_ge(x_used[es], sp.snap(doubles[es]) + 1)
                                first = nc.s_assert_within(
                                    v[2 * q] + P + c * (2 * P), 0, EP,
                                    skip_runtime_bounds_check_because="windows past the first start before EP")
                                sp.dma_start(win_x[:, es, :, :],
                                             messages[bass.ds(first, 2 * P), :]
                                             .rearrange("(k p) r -> p k r", k=2)).then_inc(s_winx[es], 16)
                                sp.reg_add(doubles[es], doubles[es], 1)
                o = s.back(6)
                if o.exists(NB):
                    sp.wait_ge(n_y, o.n + 1)
                    sp.dma_start(out_rows[bass.ds(o.n, 1), :, :, :].rearrange("a p q f -> (a p) q f"),
                                 y[:, o.slot % R, :, :].rearrange("p (q k) d -> p q (k d)", q=2)).then_inc(s_out[o.slot % R], 16)

            run_blocks(sp, NB, 6, node_step)
            for i in range(R):
                sp.wait_ge(s_out[i], 16 * len(range(i, NB, R)))

        @block.gpsimd
        def _(pool):
            nc.gpsimd.memset(pad_rows[:, :, :], -1.0).then_inc(s_fill, 1)
            pool.wait_ge(s_idx, 16)

            def edge_step(s):
                free = s.back(U)
                if free.exists(EB):
                    pool.wait_ge(e_norm, free.n + 1)
                nc.gpsimd.tensor_copy(idx[:, s.slot, :], src_sb[:, bass.ds(s.n * G, G)]).then_inc(e_idx, 1)
                wait_ahead(pool, e_idx, s.n + 1)
                for g in range(G):
                    pool.indirect_dma_start(
                        out=xg[:, s.slot, g, :], out_offset=None, in_=x,
                        in_offset=bass.IndirectOffsetOnAxis(ap=idx[:, s.slot, g:g + 1], axis=0),
                    ).then_inc(s_gather[s.slot], 16)

            run_blocks(pool, EB, 0, edge_step)

            pool.wait_ge(s_w, 160)

            def node_step(s):
                pool.wait_ge(n_norm, s.n + 1)
                nc.gpsimd.tensor_tensor(xb[:, s.slot, :, :], xb[:, s.slot, :, :],
                                        beta_bc[:, :].unsqueeze(1).to_broadcast([P, G, D]), ALU.add).then_inc(n_xb, 1)

            run_blocks(pool, NB, 0, node_step)

        @block.scalar
        def _(act):
            act.wait_ge(s_w, 160)
            act.wait_ge(s_cst, 16)

            def standard_deviation(to, of):
                return nc.scalar.activation(to, of, ACT.Sqrt, bias=cst[:, C_EPS:C_EPS + 1])

            def edge_step(s):
                if s.exists(EB):
                    act.wait_ge(e_mom, s.n + 1)
                    standard_deviation(std[:, s.slot % R, :], moments[:, s.slot % R, :, 1]).then_inc(e_std, 1)
                h = s.back(1)
                if h.exists(EB):
                    act.wait_ge(e_tr, h.n + 1)
                    if h.back(2).exists(EB):
                        act.wait_ge(e_z, h.back(2).n + 1)
                    nc.scalar.activation(hT[:, h.slot % 2, :], ps_t[h.slot % 2][:, :], ACT.Relu).then_inc(e_h, 1)
                z = s.back(2)
                if z.exists(EB):
                    act.wait_ge(e_z, z.n + 1)
                    if z.back(2).exists(EB):
                        act.wait_ge(e_m, z.back(2).n + 1)
                    nc.scalar.activation(tT[:, z.slot % 2, :], ps_z[z.slot % 2][:, :], ACT.Relu, bias=b1_col[:, 0:1])\
                      .then_inc(e_t, 1)

            run_blocks(act, EB, 2, edge_step)

            def node_step(s):
                if s.exists(NB):
                    act.wait_ge(n_mom, s.n + 1)
                    standard_deviation(std[:, s.slot % R, :], moments[:, s.slot % R, :, 1]).then_inc(n_std, 1)
                h = s.back(1)
                if h.exists(NB):
                    act.wait_ge(n_tr, h.n + 1)
                    if h.back(2).exists(NB):
                        act.wait_ge(n_u, h.back(2).n + 1)
                    else:
                        act.wait_ge(e_z, EB)
                    nc.scalar.activation(hT[:, h.slot % 2, :], ps_t[h.slot % 2][:, :], ACT.Relu).then_inc(n_h, 1)
                f = s.back(3)
                if f.exists(NB):
                    act.wait_ge(n_mom2, f.n + 1)
                    standard_deviation(std2[:, f.slot % R, :], moments2[:, f.slot % R, :, 1]).then_inc(n_std2, 1)
                u = s.back(2)
                if u.exists(NB):
                    act.wait_ge(n_u, u.n + 1)
                    if u.back(R).exists(NB):
                        act.wait_ge(n_y, u.back(R).n + 1)
                    nc.scalar.activation(r[:, u.slot % R, :, :].rearrange("p g d -> p (g d)"), ps_m[u.slot % 2][:, :],
                                         ACT.Relu).then_inc(n_r, 1)

            run_blocks(act, NB, 3, node_step)

        @block.vector
        def _(dve):
            chain = [0]

            def link(ins):
                chain[0] += 1
                ins.then_inc(s_set, 1)
                dve.wait_ge(s_set, chain[0])

            nc.vector.memset(msg[:, :, :, :], 0.0)
            link(nc.vector.memset(ones[:, :], 1.0))
            dve.wait_ge(s_w, 160)
            dve.wait_ge(s_cst, 16)
            nc.vector.tensor_copy(pick_rows[:, :], cst[:, C_ROWS:C_ROWS + P])
            link(nc.vector.tensor_copy(bs_hi[:, :], bs_bc[:, :]))
            nc.vector.tensor_copy(bs_parts[0:32, :], bs_hi[0:32, :])
            link(nc.vector.tensor_tensor(bs_rest[:, :], bs_bc[:, :], bs_hi[:, :], ALU.subtract))
            link(nc.vector.tensor_copy(bs_hi[:, :], bs_rest[:, :]))
            nc.vector.tensor_copy(bs_parts[32:64, :], bs_hi[32:64, :])
            link(nc.vector.tensor_tensor(bs_rest[:, :], bs_rest[:, :], bs_hi[:, :], ALU.subtract))
            nc.vector.tensor_copy(bs_parts[64:96, :], bs_rest[64:96, :])
            nc.vector.tensor_copy(bs_parts[96:128, :], bs_rest[96:128, :]).then_inc(s_bias, 1)
            dve.wait_ge(s_lists, 32)
            nc.vector.tensor_scalar(q_int[:, 0, :], dst_sb[:, :], PAIR_BITS + QL_BITS, None, ALU.arith_shift_right)
            nc.vector.tensor_scalar(q_int[:, 1, :], dst_sb[:, :], PAIR_BITS, QL - 1, ALU.arith_shift_right,
                                    ALU.bitwise_and)
            nc.vector.tensor_copy(dst_f[:, :], dst_sb[:, :])
            link(nc.vector.tensor_copy(next_f[:, :], next_sb[:, :]))
            nc.vector.tensor_copy(q_f[:, :, :], q_int[:, :, :])
            link(nc.vector.tensor_tensor(next_f[:, :], next_f[:, :], dst_f[:, :], ALU.is_lt))
            nc.vector.tensor_reduce(falls[:, 0:1], next_f[:, :], axis=AX.X, op=ALU.add)
            nc.vector.tensor_reduce(falls[:, 1:2], next_f[:, :], axis=AX.X, op=ALU.add)
            for hot, k, n in ((hot_h, 0, QH), (hot_l, 1, QL)):
                last = nc.vector.tensor_tensor(hot[:, :, :], q_f[:, k, :].unsqueeze(2).to_broadcast([P, ET, n]),
                                               cst[:, C_QL:C_QL + n].unsqueeze(1).to_broadcast([P, ET, n]), ALU.is_equal)
            last.then_inc(s_hot, 1)

            def edge_step(s):
                if s.exists(EB):
                    dve.wait_ge(s_gather[s.slot], (s.turn + 1) * (16 * G))
                    for g in range(G):
                        last = nc.vector.bn_stats(stats[:, s.slot % 2, g, :], xg[:, s.slot, g, :])
                    last.then_inc(e_stats, 1)
                n = s.back(1)
                if n.exists(EB):
                    if n.back(2).exists(EB):
                        dve.wait_ge(e_tr, n.back(2).n + 1)
                    dve.wait_ge(e_std, n.n + 1)
                    nc.vector.reciprocal(rstd[:, n.slot % 2, :], std[:, n.slot % R, :]).then_inc(e_rstd, 1)
                if s.exists(EB):
                    wait_ahead(dve, e_stats, s.n + 1)
                    for g in range(G):
                        last = nc.vector.bn_aggr(moments[:, s.slot % R, g, :], stats[:, s.slot % 2, g, :])
                    last.then_inc(e_mom, 1)
                if n.exists(EB):
                    dve.wait_ge(e_rstd, n.n + 1)
                    for g in range(G):
                        last = nc.vector.tensor_scalar(xn[:, n.slot % 2, g, :], xg[:, n.slot, g, :],
                                                       moments[:, n.slot % R, g, 0:1], rstd[:, n.slot % 2, g:g + 1],
                                                       ALU.subtract, ALU.mult)
                    last.then_inc(e_norm, 1)
                    dve.wait_ge(s_ty[n.slot % R], (n.use(R) + 1) * 16)
                    if n.back(R).exists(EB):
                        dve.wait_ge(e_z, n.back(R).n + 1)
                    nc.vector.tensor_scalar(ez[0:TYPES, n.slot % R, :], ty[:, n.slot % R, :], type_id[:, 0:1], None,
                                            ALU.is_equal).then_inc(e_type, 1)
                m = s.back(4)
                if m.exists(EB):
                    dve.wait_ge(e_m, m.n + 1)
                    if m.back(R).exists(EB):
                        dve.wait_ge(s_mst[m.slot % R], m.use(R) * 16)
                    nc.vector.tensor_copy(msg[:, m.slot % R, :, DST], dst_f[:, bass.ds(m.n * G, G)])
                    nc.vector.tensor_tensor(msg[:, m.slot % R, :, 0:D],
                                            ps_m[m.slot % 2][:, :].rearrange("p (g d) -> p g d", g=G),
                                            b2_bc[:, :].unsqueeze(1).to_broadcast([P, G, D]), ALU.add).then_inc(e_msg, 1)

            type_id = cst[0:TYPES, C_TYPE:C_TYPE + 1]
            run_blocks(dve, EB, 4, edge_step)

            dve.wait_ge(s_hist, 1)
            nc.vector.tensor_copy(count[:, :], ps_q[:, 0:QL])
            link(nc.vector.tensor_scalar(is_sorted[:, :], ps_q[:, QL:QL + 2], 1.0, None, ALU.is_equal))
            link(nc.vector.tensor_tensor_scan(upto[:, :], ones[0:QH, 0:QL], count[:, :], 0.0, ALU.mult, ALU.add))
            nc.vector.tensor_copy(total[:, :], upto[:, QL - 1:QL].to_broadcast([QH, 2])).then_inc(s_tot, 1)
            dve.wait_ge(s_off, 1)
            link(nc.vector.tensor_copy(offset[:, :], ps_q[:, QL + 2:QL + 4]))
            link(nc.vector.tensor_tensor(upto[:, :], upto[:, :], count[:, :], ALU.subtract))
            nc.vector.tensor_scalar(tab_f[:, :, 0], upto[:, :], offset[:, 0:1], is_sorted[:, 0:1], ALU.add, ALU.mult)
            link(nc.vector.tensor_scalar(total[:, :], is_sorted[:, :], -float(EP), float(EP), ALU.mult, ALU.add))
            link(nc.vector.tensor_scalar(tab_f[:, :, 1], count[:, :], total[:, 0:1], float(P - 1), ALU.max, ALU.add))
            link(nc.vector.tensor_copy(tab_i[:, :, :], tab_f[:, :, :]))
            nc.vector.tensor_scalar(tab_i[:, :, 1], tab_i[:, :, 1], 8, None, ALU.arith_shift_right).then_inc(s_tabi, 1)

            dve.wait_ge(s_tab, 16)
            doubles = [dve.alloc_register(f"dve_doubles{i}") for i in range(4)]
            for reg in doubles:
                dve.reg_mov(reg, 0)

            def select(s, q, to, window):
                return nc.vector.tensor_scalar(to, slot_of, window[:, DST:DST + 1],
                                               cst[:, bass.ds(s.n * 2 + C_BASE + q, 1)], ALU.subtract, ALU.is_equal)

            def node_step(s):
                if s.exists(NB):
                    dve.wait_ge(s_x[s.slot], (s.turn + 1) * 16)
                    for g in range(G):
                        last = nc.vector.bn_stats(stats[:, s.slot % 2, g, :], xb[:, s.slot, g, :])
                    last.then_inc(n_stats, 1)
                n = s.back(1)
                if n.exists(NB):
                    if n.back(2).exists(NB):
                        dve.wait_ge(n_tr, n.back(2).n + 1)
                    else:
                        dve.wait_ge(e_tr, EB)
                    dve.wait_ge(n_std, n.n + 1)
                    nc.vector.reciprocal(rstd[:, n.slot % 2, :], std[:, n.slot % R, :]).then_inc(n_rstd, 1)
                if s.exists(NB):
                    wait_ahead(dve, n_stats, s.n + 1)
                    for g in range(G):
                        last = nc.vector.bn_aggr(moments[:, s.slot % R, g, :], stats[:, s.slot % 2, g, :])
                    last.then_inc(n_mom, 1)
                if n.exists(NB):
                    dve.wait_ge(n_rstd, n.n + 1)
                    for g in range(G):
                        last = nc.vector.tensor_scalar(xn[:, n.slot % 2, g, :], xb[:, n.slot, g, :],
                                                       moments[:, n.slot % R, g, 0:1], rstd[:, n.slot % 2, g:g + 1],
                                                       ALU.subtract, ALU.mult)
                    last.then_inc(n_norm, 1)
                f = s.back(3)
                if f.exists(NB):
                    dve.wait_ge(n_r, f.n + 1)
                    for g in range(G):
                        last = nc.vector.bn_stats(stats2[:, f.slot % 2, g, :], r[:, f.slot % R, g, :])
                    last.then_inc(n_stats2, 1)
                w = s.back(2)
                if w.exists(NB):
                    v = load_table(dve, w)
                    dve.wait_ge(s_win[w.slot % R], (w.use(R) + 1) * 32)
                    if w.back(2).exists(NB):
                        dve.wait_ge(n_u, w.back(2).n + 1)
                    for q in range(2):
                        last = select(w, q, sel[:, w.slot % 2, q, :], win[:, w.slot % R, q, :])
                    last.then_inc(n_sel, 1)
                    for q in range(2):
                        es = extra_slot(w, q)
                        with dve.If(v[2 * q + 1] > 0):
                            with dve.Fori(0, v[2 * q + 1]):
                                done = dve.snap(doubles[es])
                                dve.wait_ge(s_winx[es], (done + 1) * 16)
                                dve.wait_ge(x_used[es], done + 1)
                                for i in range(2):
                                    last = select(w, q, sel_x[:, es, i, :], win_x[:, es, i, :])
                                last.then_inc(x_sel[es], 1)
                                dve.reg_add(doubles[es], doubles[es], 1)
                if f.exists(NB):
                    wait_ahead(dve, n_stats2, f.n + 1)
                    for g in range(G):
                        last = nc.vector.bn_aggr(moments2[:, f.slot % R, g, :], stats2[:, f.slot % 2, g, :])
                    last.then_inc(n_mom2, 1)
                o = s.back(4)
                if o.exists(NB):
                    if o.back(2).exists(NB):
                        dve.wait_ge(n_y, o.back(2).n + 1)
                    dve.wait_ge(n_std2, o.n + 1)
                    nc.vector.reciprocal(rstd2[:, o.slot % 2, :], std2[:, o.slot % R, :]).then_inc(n_rstd2, 1)
                    for g in range(G):
                        last = nc.vector.scalar_tensor_tensor(r[:, o.slot % R, g, :], r[:, o.slot % R, g, :],
                                                              moments2[:, o.slot % R, g, 0:1], gamma_bc[:, :],
                                                              ALU.subtract, ALU.mult)
                    last.then_inc(n_cen, 1)
                    dve.wait_ge(n_xb, o.n + 1)
                    if o.back(R).exists(NB):
                        dve.wait_ge(s_out[o.slot % R], o.use(R) * 16)
                    dve.wait_ge(n_rstd2, o.n + 1)
                    dve.wait_ge(n_cen, o.n + 1)
                    for g in range(G):
                        last = nc.vector.scalar_tensor_tensor(y[:, o.slot % R, g, :], r[:, o.slot % R, g, :],
                                                              rstd2[:, o.slot % 2, g:g + 1], xb[:, o.slot, g, :], ALU.mult, ALU.add)
                    last.then_inc(n_y, 1)

            run_blocks(dve, NB, 4, node_step)

        @block.tensor
        def _(pe):
            pe.wait_ge(s_hot, 1)
            HU = 4
            hist = ps_q[:, 0:QL]
            for t in range(HU):
                nc.tensor.matmul(hist, hot_h[:, t, :], hot_l[:, t, :], start=(t == 0), stop=False)
            with pe.Fori(1, ET // HU - 1) as i:
                for t in range(HU):
                    nc.tensor.matmul(hist, hot_h[:, bass.ds(i * HU + t, 1), :].rearrange("p a b -> p (a b)"),
                                     hot_l[:, bass.ds(i * HU + t, 1), :].rearrange("p a b -> p (a b)"),
                                     start=False, stop=False)
            for t in range(ET - HU, ET):
                nc.tensor.matmul(hist, hot_h[:, t, :], hot_l[:, t, :], start=False, stop=(t == ET - 1))
            nc.tensor.matmul(ps_q[:, QL:QL + 2], ones[:, 0:QH], falls[:, :], start=True, stop=True).then_inc(s_hist, 1)
            pe.wait_ge(s_w, 160)
            pe.wait_ge(s_cst, 16)

            def edge_step(s):
                if s.exists(EB):
                    pe.wait_ge(e_norm, s.n + 1)
                    if s.back(2).exists(EB):
                        pe.wait_ge(e_h, s.back(2).n + 1)
                    for g in range(G):
                        last = nc.tensor.transpose(ps_t[s.slot % 2][:, g * P:(g + 1) * P], xn[:, s.slot % 2, g, :], ident)
                    last.then_inc(e_tr, 1)
                z = s.back(1)
                if z.exists(EB):
                    pe.wait_ge(e_type, z.n + 1)
                    pe.wait_ge(s_ez[z.slot % R], (z.use(R) + 1) * 16)
                    if z.back(2).exists(EB):
                        pe.wait_ge(e_t, z.back(2).n + 1)
                    nc.tensor.matmul(ps_z[z.slot % 2][:, :], w1_e[:, :], ez[:, z.slot % R, :], start=True, stop=False)
                    pe.wait_ge(e_h, z.n + 1)
                    nc.tensor.matmul(ps_z[z.slot % 2][:, :], w1_x[:, :], hT[:, z.slot % 2, :], start=False, stop=True)\
                      .then_inc(e_z, 1)
                m = s.back(2)
                if m.exists(EB):
                    pe.wait_ge(e_t, m.n + 1)
                    if m.back(2).exists(EB):
                        pe.wait_ge(e_msg, m.back(2).n + 1)
                    for g in range(G):
                        last = nc.tensor.matmul(ps_m[m.slot % 2][:, g * D:(g + 1) * D],
                                                tT[:, m.slot % 2, g * P:(g + 1) * P], w2_sb[:, :], start=True, stop=True)
                    last.then_inc(e_m, 1)

            run_blocks(pe, EB, 2, edge_step)

            pe.wait_ge(s_tot, 1)
            nc.tensor.matmul(ps_q[:, QL + 2:QL + 4], tri[0:QH, 0:QH], total[:, :], start=True, stop=True).then_inc(s_off, 1)
            pe.wait_ge(s_bias, 1)
            pe.wait_ge(s_tab, 16)

            doubles = [pe.alloc_register(f"pe_doubles{i}") for i in range(4)]
            for reg in doubles:
                pe.reg_mov(reg, 0)
            for i in range(4):
                pe.sem_inc(x_used[i], 1)

            def node_step(s):
                if s.exists(NB):
                    pe.wait_ge(n_norm, s.n + 1)
                    if s.back(2).exists(NB):
                        pe.wait_ge(n_h, s.back(2).n + 1)
                    else:
                        pe.wait_ge(e_h, EB)
                    for g in range(G):
                        last = nc.tensor.transpose(ps_t[s.slot % 2][:, g * P:(g + 1) * P], xn[:, s.slot % 2, g, :], ident)
                    last.then_inc(n_tr, 1)
                u = s.back(1)
                if u.exists(NB):
                    v = load_table(pe, u)
                    ps_u = ps_m[u.slot % 2]
                    if u.back(2).exists(NB):
                        pe.wait_ge(n_r, u.back(2).n + 1)
                    else:
                        pe.wait_ge(e_msg, EB)
                    nc.tensor.matmul(ps_u[:, :], pick_rows[:, :], bs_parts[:, :], start=True, stop=False)
                    pe.wait_ge(n_h, u.n + 1)
                    for g in range(G):
                        nc.tensor.matmul(ps_u[:, g * D:(g + 1) * D], hT[:, u.slot % 2, g * P:(g + 1) * P], ws_sb[:, :],
                                         start=False, stop=False)
                    for q in range(2):
                        es = extra_slot(u, q)
                        with pe.If(v[2 * q + 1] > 0):
                            with pe.Fori(0, v[2 * q + 1]) as c:
                                pe.wait_ge(x_sel[es], pe.snap(doubles[es]) + 1)
                                for w in range(2):
                                    for k in range(2):
                                        g = 2 * q + k
                                        last = nc.tensor.matmul(ps_u[:, g * D:(g + 1) * D],
                                                                sel_x[:, es, w, k * P:(k + 1) * P], win_x[:, es, w, 0:D],
                                                                start=False, stop=False)
                                last.then_inc(x_used[es], 1)
                                pe.reg_add(doubles[es], doubles[es], 1)
                    pe.wait_ge(n_sel, u.n + 1)
                    for q in range(2):
                        for k in range(2):
                            g = 2 * q + k
                            last = nc.tensor.matmul(ps_u[:, g * D:(g + 1) * D], sel[:, u.slot % 2, q, k * P:(k + 1) * P],
                                                    win[:, u.slot % R, q, 0:D], start=False, stop=(g == G - 1))
                    last.then_inc(n_u, 1)

            run_blocks(pe, NB, 1, node_step)


def kernel(x, src, dst, edge_attr_16, edge_type_2, L0_gnn_W1, L0_gnn_b1, L0_gnn_W2, L0_gnn_b2, L0_gnn_Ws, L0_gnn_bs,
           L0_gnn_gamma, L0_gnn_beta):
    import concourse.bacc as bacc
    from concourse.bass_utils import run_bass_kernel_spmd

    def padded(a, rows, fill=0):
        a = np.asarray(a)
        whole = np.full((rows,) + a.shape[1:], fill, a.dtype)
        whole[:len(a)] = a
        return whole

    dst_all = padded(dst, EP + 1, -1)
    types = padded(edge_type_2, EP).reshape(P, EB, G).transpose(1, 2, 0).reshape(EB, 1, BLK)
    feats = padded(edge_attr_16, EP).reshape(P, EB, G, EF).transpose(1, 3, 2, 0).reshape(EB, EF, BLK)

    consts = np.zeros((P, C_END), np.float32)
    consts[:, C_ID:C_ID + P] = np.eye(P)
    consts[:, C_SLOT:C_SLOT + PAIR] = np.arange(PAIR).reshape(P, 2).T.reshape(1, PAIR)
    consts[:, C_BASE:C_BASE + PAIRS] = -np.arange(0, NP, PAIR)
    consts[:, C_QL:C_QL + QL] = np.arange(QL)
    consts[:, C_TRI:C_TRI + P] = np.triu(np.ones((P, P)), 1)
    consts[[0, 32, 64], C_ROWS:C_ROWS + P] = 1.0
    consts[:, C_TYPE] = np.arange(P)
    consts[:, C_EPS] = EPS

    arrays = {
        "x": padded(x, NP), "src": padded(src, EP).reshape(P, ET), "dst": dst_all[:EP].reshape(P, ET),
        "dst_next": dst_all[1:].reshape(P, ET), "types": np.repeat(types, TYPES, axis=1), "feats": feats,
        "w1": L0_gnn_W1, "b1": np.asarray(L0_gnn_b1).reshape(D, 1), "w2": L0_gnn_W2, "b2": L0_gnn_b2, "ws": L0_gnn_Ws,
        "bs": np.tile(np.asarray(L0_gnn_bs), G), "gamma": L0_gnn_gamma, "beta": L0_gnn_beta, "consts": consts,
    }
    arrays = {f"in_{k}": np.ascontiguousarray(a) for k, a in arrays.items()}
    nc = bacc.Bacc("TRN2", target_bir_lowering=False, num_devices=1)
    args = [nc.dram_tensor(k, a.shape, mybir.dt.from_np(a.dtype), kind="ExternalInput").ap() for k, a in arrays.items()]
    out = nc.dram_tensor("out", (NP, D), mybir.dt.float32, kind="ExternalOutput").ap()
    build(nc, *args, out)
    result = run_bass_kernel_spmd(nc, [arrays], core_ids=[0])
    return result.results[0]["out"][:N]
```

```python
from contextlib import ExitStack

import numpy as np

import concourse.bass as bass
from concourse import mybir

P = 128
D = 128
N = 100000
E = 50000
EF = 16
TYPES = 2
G = 4
BLK = G * P
EB = -(-E // BLK)
ET = EB * G
EP = EB * BLK
NB = -(-N // BLK)
NP = NB * BLK
PAIR = 2 * P
PAIRS = NP // PAIR
ROW = D + 4
DST = D
QL = 32
QH = -(-PAIRS // QL)
PAIR_BITS, QL_BITS = 8, 5
EPS = 1e-5
U = 12
H = 6
R = 4
DVE_TILES = 3

EXTRA_BLOCKS = 3
EXTRA_SLOTS = EXTRA_BLOCKS * 2 * 2
PACK = 16

C_ID = 0
C_SLOT = C_ID + P
C_BASE = C_SLOT + PAIR
C_QL = C_BASE + PAIRS
C_TRI = C_QL + QL
C_ROWS = C_TRI + P
C_EPS = C_ROWS + P
C_DIAG = C_EPS + 1
C_FOLD = C_DIAG + G * QL
C_END = C_FOLD + QH

SEG = ET // G

assert EB % U >= H - R
assert EP < 1 << PACK and NB % U >= 3
assert NB == 2 * EB and SEG <= P and G * QH <= P
assert 1 << PAIR_BITS == PAIR and 1 << QL_BITS == QL and QH <= P


class Step:

    def __init__(self, turn, slot):
        self.turn, self.slot = turn, slot

    @property
    def n(self):
        return self.turn * U + self.slot

    def back(self, k):
        return Step(self.turn + (self.slot - k) // U, (self.slot - k) % U)

    def use(self, ring):
        return self.turn * (U // ring) + self.slot // ring

    def is_block(self, n):
        return isinstance(self.turn, int) and self.n == n

    def exists(self, total):
        return not isinstance(self.turn, int) or 0 <= self.n < total


def run_blocks(eng, total, lag, step):
    turns = total // U
    for n in range(U):
        step(Step(n // U, n % U))
    with eng.Fori(1, turns) as turn:
        for slot in range(U):
            step(Step(turn, slot))
    for n in range(turns * U, total + lag):
        step(Step(n // U, n % U))


def build(nc, x, src, dst, dst_next, types, ef_rows, w1, b1, w2, b2, ws, bs, gamma, beta, consts, out):
    f32, bf16, i32 = mybir.dt.float32, mybir.dt.bfloat16, mybir.dt.int32
    ALU, ACT = mybir.AluOpType, mybir.ActivationFunctionType
    AX = mybir.AxisListType

    messages = nc.dram_tensor("messages", (EP + 2 * P, ROW), f32, kind="Internal").ap()
    hot_types = nc.dram_tensor("hot_types", (TYPES, ET, P), f32, kind="Internal").ap()
    msg_store = messages[0:EP, :].rearrange("(p b g) r -> b p g r", p=P, g=G)
    x_rows = x.rearrange("(b q p k) d -> b p q (k d)", q=2, p=P, k=2)
    out_rows = out.rearrange("(b q p k) d -> b p q (k d)", q=2, p=P, k=2)

    ctx = ExitStack()
    with ctx:
        def sb(name, shape, dt=f32):
            return ctx.enter_context(nc.sbuf_tensor(name, shape, dt))

        def pb(name, shape, dt=f32):
            return ctx.enter_context(nc.psum_tensor(name, shape, dt))

        def sem(name):
            return ctx.enter_context(nc.semaphore(name))

        cst = sb("cst", [P, C_END])
        ident = cst[:, C_ID:C_ID + P]
        slot_of = cst[:, C_SLOT:C_SLOT + PAIR]
        tri = cst[:, C_TRI:C_TRI + P]
        w1_x = sb("w1_x", [D, D])
        w1_e = sb("w1_e", [TYPES + EF, D])
        w2_sb = sb("w2_sb", [D, D])
        ws_sb = sb("ws_sb", [D, D])
        b1_col = sb("b1_col", [D, 1])
        b2_bc = sb("b2_bc", [P, BLK])
        b2_parts = sb("b2_parts", [P, BLK], bf16)
        bs_bc = sb("bs_bc", [P, BLK])
        gamma_bc = sb("gamma_bc", [P, D])
        beta_bc = sb("beta_bc", [P, D])
        pick_rows = sb("pick_rows", [P, P], bf16)
        bs_parts = sb("bs_parts", [P, BLK], bf16)
        bias_hi = sb("bias_hi", [P, BLK], bf16)
        dst_sb = sb("dst_sb", [P, ET], i32)
        next_sb = sb("next_sb", [P, ET], i32)
        dst_f = sb("dst_f", [P, ET])
        next_f = sb("next_f", [P, ET])
        q_int = sb("q_int", [P, 2, ET], i32)
        q_f = sb("q_f", [P, 2, ET])
        hot_h = sb("hot_h", [P, 2, G, QH], bf16)
        hot_l = sb("hot_l", [P, 2, G, QL], bf16)
        type_sb = sb("type_sb", [P, ET], i32)
        type_hot = sb("type_hot", [P, TYPES, ET])
        type_turned = sb("type_turned", [SEG, TYPES, G * P])
        counts = sb("counts", [G * QH, G * QL])
        falls = sb("falls", [P, 2])
        ones = sb("ones", [P, P])
        count = sb("count", [QH, QL])
        upto = sb("upto", [QH, QL])
        total = sb("total", [QH, 2])
        offset = sb("offset", [QH, 2])
        is_sorted = sb("is_sorted", [QH, 2])
        tab_f = sb("tab_f", [QH, 2, QL])
        tab_i = sb("tab_i", [QH, 2, QL], i32)
        tab_packed = sb("tab_packed", [QH, QL], i32)
        table = sb("table", [1, QH * QL], i32)
        pad_rows = sb("pad_rows", [P, 2, ROW])
        xg = sb("xg", [P, H, G, D])
        idx = sb("idx", [P, H, G], i32)
        ez = sb("ez", [TYPES + EF, R, BLK])
        msg = sb("msg", [P, R, G, ROW])
        stats = sb("stats", [P, 2, G, 6])
        shift = sb("shift", [P, 2, G])
        x_stats = sb("x_stats", [P, 2, 2 * G, 6])
        x_moments = sb("x_moments", [P, R, 2 * G, 2])
        x_std = sb("x_std", [P, 2, 2 * G])
        x_rstd = sb("x_rstd", [P, NB * G])
        x_shift = sb("x_shift", [P, NB * G])
        moments = sb("moments", [P, R, G, 2])
        std = sb("std", [P, R, G])
        rstd = sb("rstd", [P, 2, G])
        xn = sb("xn", [P, 2, G, D])
        hT = sb("hT", [D, 2, BLK])
        tT = sb("tT", [D, 2, BLK])
        xb = sb("xb", [P, U, G, D])
        win = sb("win", [P, R, 2, ROW])
        rel = sb("rel", [P, R, 2])
        sel = sb("sel", [P, 2, 2, PAIR])
        win_x = sb("win_x", [P, EXTRA_SLOTS, 2, ROW])
        sel_x = sb("sel_x", [P, EXTRA_SLOTS, 2, PAIR])
        r = sb("r", [P, H, G, D])
        stats2 = sb("stats2", [P, 2, G, 6])
        moments2 = sb("moments2", [P, R, G, 2])
        std2 = sb("std2", [P, R, G])
        rstd2 = sb("rstd2", [P, R, G])
        shift2 = sb("shift2", [P, R, G])
        y = sb("y", [P, R, G, D])

        ps_t = [pb(f"ps_t{i}", [D, BLK]) for i in range(2)]
        ps_z = [pb(f"ps_z{i}", [D, BLK]) for i in range(2)]
        ps_m = [pb(f"ps_m{i}", [P, BLK]) for i in range(2)]
        ps_q = pb("ps_q", [QH, BLK])
        ps_h = pb("ps_h", [G * QH, G * QL])

        s_idx = [sem(f"src_loaded{i}") for i in range(H)]
        s_lists = sem("dst_loaded")
        s_cst = sem("consts_loaded")
        s_w = sem("weights_loaded")
        s_gather = [sem(f"gathered{i}") for i in range(H)]
        s_ez = [sem(f"edge_feats_loaded{i}") for i in range(R)]
        s_types = sem("types_list_loaded")
        s_turned = sem("types_turned_stored")
        s_xa = [sem(f"x_loaded_for_stats{i}") for i in range(U)]
        s_mst = [sem(f"messages_stored{i}") for i in range(R)]
        s_pad = sem("pad_rows_stored")
        s_tab = sem("table_ready")
        s_x = [sem(f"x_loaded{i}") for i in range(U)]
        s_win = [sem(f"windows_loaded{i}") for i in range(R)]
        s_winx = [sem(f"extra_windows_loaded{i}") for i in range(EXTRA_SLOTS)]
        s_out = [sem(f"out_stored{i}") for i in range(R)]
        s_set = sem("setup_chain")
        s_passed = sem("waits_passed")
        s_fill = sem("fills_done")
        s_bias = sem("bias_parts_ready")
        s_falls = sem("falls_counted_by_row")
        e_hot = sem("pair_one_hots")
        e_hist = sem("histogram_added")
        s_thot = sem("types_hot")
        s_ttr = sem("types_transposed")
        s_tcp = sem("types_turned")
        s_hist = sem("histogram_ready")
        s_folded = sem("histogram_masked")
        s_tot = sem("totals_ready")
        s_off = sem("offsets_ready")
        s_tabi = sem("table_computed")
        e_stats = sem("edge_stats")
        e_mom = sem("edge_moments")
        e_std = sem("edge_std")
        e_rstd = sem("edge_rstd")
        e_norm = sem("edge_normed")
        x_st = sem("x_block_stats")
        x_mo = sem("x_block_moments")
        x_sd = sem("x_block_std")
        x_inv = sem("x_block_inverse_std")
        x_fac = sem("x_block_rstd_shift")
        e_rinv = sem("edge_inverse_std")
        e_tr = sem("edge_transposed")
        e_h = sem("edge_hT")
        e_z = sem("edge_z")
        e_t = sem("edge_tT")
        e_m = sem("edge_m")
        e_msg = sem("edge_msg")
        e_dst = sem("edge_msg_dst")
        n_norm = sem("node_normed")
        n_tr = sem("node_transposed")
        n_h = sem("node_hT")
        n_sel = sem("node_sel")
        n_xb = sem("node_x_beta")
        n_u = sem("node_u")
        n_r = sem("node_r")
        n_stats2 = sem("node_stats2")
        n_mom2 = sem("node_moments2")
        n_std2 = sem("node_std2")
        n_rstd2 = sem("node_rstd2")
        n_fac2 = sem("node_rstd2_shift2")
        n_ln = [sem(f"node_normalised{i}") for i in range(2)]
        n_gam = sem("node_times_gamma")
        n_rel = sem("node_rel")
        n_y = sem("node_y")
        x_sel = [sem(f"extra_sel{i}") for i in range(EXTRA_SLOTS)]
        x_used = [sem(f"extra_used{i}") for i in range(EXTRA_SLOTS)]

        def for_extras(eng, s, entries, doubles, one):
            with eng.If((entries[0] | entries[1]) >= 1 << PACK):
                for q in range(2):
                    for_pair_extras(eng, 4 * (s.slot % EXTRA_BLOCKS) + 2 * q, entries[q] >> PACK, doubles,
                                    lambda es, c: one(q, es, c))

        def for_pair_extras(eng, es, count, doubles, one):
            with eng.If(count > 0):
                one(es, 0)
                eng.reg_add(doubles[es], doubles[es], 1)
                with eng.If(count > 1):
                    one(es + 1, 1)
                    eng.reg_add(doubles[es + 1], doubles[es + 1], 1)
                    with eng.If(count > 2):
                        with eng.Fori(2, count, 2) as c:
                            one(es, c)
                            eng.reg_add(doubles[es], doubles[es], 1)
                            with eng.If(c + 1 < count):
                                one(es + 1, c + 1)
                                eng.reg_add(doubles[es + 1], doubles[es + 1], 1)

        def running_counts(eng, name):
            doubles = [eng.alloc_register(f"{name}_doubles{i}") for i in range(EXTRA_SLOTS)]
            for reg in doubles:
                eng.reg_mov(reg, 0)
            return doubles

        def wait_ahead(eng, semaphore, value):
            eng.wait_ge(semaphore, value)
            eng.sem_inc(s_passed, 1)

        def load_table(eng, s):
            row = table[0:1, bass.ds(s.n * 2, 2)]
            _, v = nc.values_load_multi_w_load_instructions(
                row, engines=[eng.engine], min_val=0, max_val=(EP >> 7) << PACK,
                skip_runtime_bounds_check_because="first edges and counts are at most EP by the table's construction")
            return v

        block = ctx.enter_context(nc.Block())

        @block.sync
        def _(sp):
            def load_src(s):
                sp.dma_start(idx[:, s.slot % H, :], src[:, bass.ds(s.n * G, G)]).then_inc(s_idx[s.slot % H], 16)

            for n in range(H):
                load_src(Step(0, n))
            sp.dma_start(type_sb[:, :], types).then_inc(s_types, 16)
            sp.dma_start(dst_sb[:, :], dst).then_inc(s_lists, 16)
            sp.dma_start(next_sb[:, :], dst_next).then_inc(s_lists, 16)
            sp.dma_start(cst[:, :], consts).then_inc(s_cst, 16)
            sp.dma_start(w1_x[:, :], w1[0:D, :]).then_inc(s_w, 16)
            sp.dma_start(w1_e[0:TYPES, :], w1[D + EF:D + EF + TYPES, :]).then_inc(s_w, 16)
            sp.dma_start(w1_e[TYPES:TYPES + EF, :], w1[D:D + EF, :]).then_inc(s_w, 16)
            sp.dma_start(w2_sb[:, :], w2).then_inc(s_w, 16)
            sp.dma_start(b1_col[:, :], b1).then_inc(s_w, 16)
            sp.dma_start(b2_bc[:, :], b2.partition_broadcast(P)).then_inc(s_w, 16)
            sp.dma_start(ws_sb[:, :], ws).then_inc(s_w, 16)
            sp.dma_start(bs_bc[:, :], bs.partition_broadcast(P)).then_inc(s_w, 16)
            sp.dma_start(gamma_bc[:, :], gamma.partition_broadcast(P)).then_inc(s_w, 16)
            sp.dma_start(beta_bc[:, :], beta.partition_broadcast(P)).then_inc(s_w, 16)

            sp.wait_ge(s_tcp, 1)
            for k in range(TYPES):
                sp.dma_start(hot_types[k].rearrange("(c t) p -> t c p", c=G),
                             type_turned[:, k, :].rearrange("t (c p) -> t c p", c=G)).then_inc(s_turned, 16)
            sp.wait_ge(s_turned, 16 * TYPES)

            def load_x(ring, slot, n):
                sp.dma_start(xb[:, slot, :, :].rearrange("p (q k) d -> p q (k d)", q=2),
                             x_rows[bass.ds(n, 1), :, :, :].rearrange("a p q f -> (a p) q f")).then_inc(ring[slot], 16)

            sp.wait_ge(s_fill, 1)
            sp.dma_start(messages[EP:EP + 2 * P, :].rearrange("(p k) r -> p k r", k=2), pad_rows[:, :, :])\
              .then_inc(s_pad, 16)

            def edge_step(s):
                if s.exists(EB):
                    if s.back(R).exists(EB):
                        sp.wait_ge(e_z, s.back(R).n + 1)
                    a = s.back(R - H)
                    if s.back(R).exists(EB) and a.exists(EB):
                        load_src(a)
                    sp.dma_start(ez[0:TYPES, s.slot % R, :].rearrange("k (t p) -> k t p", t=G),
                                 hot_types[:, bass.ds(s.n * G, G), :]).then_inc(s_ez[s.slot % R], 16)
                    sp.dma_start(ez[TYPES:, s.slot % R, :], ef_rows[bass.ds(s.n, 1), :, :].rearrange("a t e -> (a t) e"))\
                      .then_inc(s_ez[s.slot % R], 16)
                    if s.back(R).exists(EB):
                        sp.wait_ge(x_mo, s.back(R).n + 1)
                    for i in range(2):
                        load_x(s_xa, (2 * s.slot + i) % U, s.n * 2 + i)
                if s.is_block(EB + 1):
                    sp.wait_ge(x_mo, EB)
                    for n in range(U):
                        load_x(s_x, n, n)
                m = s.back(6)
                if m.exists(EB):
                    sp.wait_ge(e_msg, m.n + 1)
                    sp.wait_ge(e_dst, m.n + 1)
                    sp.dma_start(msg_store[bass.ds(m.n, 1), :, :, :].rearrange("a p g r -> (a p) g r"),
                                 msg[:, m.slot % R, :, :]).then_inc(s_mst[m.slot % R], 16)

            run_blocks(sp, EB, 6, edge_step)
            sp.wait_ge(s_tabi, 1)
            sp.dma_start(table[:, :].rearrange("o (a b) -> o a b", a=QH), tab_packed[:, :]).then_inc(s_tab, 16)
            sp.wait_ge(s_tab, 16)
            sp.wait_ge(s_pad, 16)
            for i in range(R):
                sp.wait_ge(s_mst[i], 16 * len(range(i, EB, R)))

            doubles = running_counts(sp, "sp")

            def node_step(s):
                o = s.back(9)
                if o.exists(NB):
                    sp.wait_ge(n_y, o.n + 1)
                    sp.dma_start(out_rows[bass.ds(o.n, 1), :, :, :].rearrange("a p q f -> (a p) q f"),
                                 y[:, o.slot % R, :, :].rearrange("p (q k) d -> p q (k d)", q=2)).then_inc(s_out[o.slot % R], 16)
                if s.exists(NB) and s.back(R).exists(NB):
                    sp.wait_ge(n_u, s.back(R).n + 1)
                if o.exists(NB):
                    ahead = o.back(-U)
                    if ahead.exists(NB):
                        load_x(s_x, ahead.slot, ahead.n)
                if s.exists(NB):
                    entries = load_table(sp, s)
                    first = [nc.s_assert_within(sp.snap(v & (1 << PACK) - 1), 0, EP,
                                                skip_runtime_bounds_check_because="a first edge is at most EP")
                             for v in entries]
                    for q in range(2):
                        sp.dma_start(win[:, s.slot % R, q, :], messages[bass.ds(first[q], P), :])\
                          .then_inc(s_win[s.slot % R], 16)

                    def load(q, es, c):
                        start = nc.s_assert_within(
                            sp.snap(first[q] + P + c * (2 * P)), 0, EP,
                            skip_runtime_bounds_check_because="windows past the first start before EP")
                        sp.wait_ge(x_used[es], sp.snap(doubles[es]) + 1)
                        sp.dma_start(win_x[:, es, :, :], messages[bass.ds(start, 2 * P), :]
                                     .rearrange("(k p) r -> p k r", k=2)).then_inc(s_winx[es], 16)

                    for_extras(sp, s, entries, doubles, load)

            run_blocks(sp, NB, 9, node_step)
            for i in range(R):
                sp.wait_ge(s_out[i], 16 * len(range(i, NB, R)))

        @block.gpsimd
        def _(pool):
            nc.gpsimd.memset(pad_rows[:, :, :], -1.0).then_inc(s_fill, 1)

            def edge_step(s):
                free = s.back(H)
                if free.exists(EB):
                    pool.wait_ge(e_norm, free.n + 1)
                wait_ahead(pool, s_idx[s.slot % H], (s.use(H) + 1) * 16)
                for g in range(G):
                    pool.indirect_dma_start(
                        out=xg[:, s.slot % H, g, :], out_offset=None, in_=x,
                        in_offset=bass.IndirectOffsetOnAxis(ap=idx[:, s.slot % H, g:g + 1], axis=0),
                    ).then_inc(s_gather[s.slot % H], 16)

            run_blocks(pool, EB, 0, edge_step)

            pool.wait_ge(s_w, 160)

            def node_step(s):
                if s.exists(NB):
                    pool.wait_ge(s_win[s.slot % R], (s.use(R) + 1) * 32)
                    if s.back(R).exists(NB):
                        pool.wait_ge(n_sel, s.back(R).n + 1)
                    nc.gpsimd.tensor_tensor(rel[:, s.slot % R, :], win[:, s.slot % R, :, DST],
                                            cst[:, bass.ds(s.n * 2 + C_BASE, 2)], ALU.add).then_inc(n_rel, 1)
                b = s.back(1)
                if b.exists(NB):
                    pool.wait_ge(n_norm, b.n + 1)
                    nc.gpsimd.tensor_tensor(xb[:, b.slot, :, :], xb[:, b.slot, :, :],
                                            beta_bc[:, :].unsqueeze(1).to_broadcast([P, G, D]), ALU.add)\
                      .then_inc(n_xb, 1)
                o = s.back(5)
                if o.exists(NB):
                    for sem_ in n_ln:
                        pool.wait_ge(sem_, o.n + 1)
                    nc.gpsimd.tensor_tensor(r[:, o.slot % H, :, :], r[:, o.slot % H, :, :],
                                            gamma_bc[:, :].unsqueeze(1).to_broadcast([P, G, D]), ALU.mult)\
                      .then_inc(n_gam, 1)

            run_blocks(pool, NB, 5, node_step)

        @block.scalar
        def _(act):
            act.wait_ge(s_w, 160)
            act.wait_ge(s_cst, 16)

            def standard_deviation(to, of):
                return nc.scalar.activation(to, of, ACT.Sqrt, bias=cst[:, C_EPS:C_EPS + 1])

            def normalise(to, of, scale, shift_):
                return nc.scalar.activation(to, of, ACT.Identity, bias=shift_, scale=scale)

            def edge_step(s):
                k = s.back(1)
                if k.exists(EB):
                    act.wait_ge(x_mo, k.n + 1)
                    if k.back(2).exists(EB):
                        act.wait_ge(x_fac, k.back(2).n + 1)
                    standard_deviation(x_std[:, k.slot % 2, :], x_moments[:, k.slot % R, :, 1]).then_inc(x_sd, 1)
                if s.exists(EB):
                    act.wait_ge(e_mom, s.n + 1)
                    if s.back(R).exists(EB):
                        act.wait_ge(e_rstd, s.back(R).n + 1)
                    standard_deviation(std[:, s.slot % R, :], moments[:, s.slot % R, :, 1]).then_inc(e_std, 1)
                n = s.back(1)
                if n.exists(EB):
                    act.wait_ge(e_rstd, n.n + 1)
                    if n.back(2).exists(EB):
                        act.wait_ge(e_tr, n.back(2).n + 1)
                    for g in range(G):
                        last = normalise(xn[:, n.slot % 2, g, :], xg[:, n.slot % H, g, :], rstd[:, n.slot % 2, g:g + 1],
                                         shift[:, n.slot % 2, g:g + 1])
                    last.then_inc(e_norm, 1)
                h = s.back(2)
                if h.exists(EB):
                    act.wait_ge(e_tr, h.n + 1)
                    if h.back(2).exists(EB):
                        act.wait_ge(e_z, h.back(2).n + 1)
                    nc.scalar.activation(hT[:, h.slot % 2, :], ps_t[h.slot % 2][:, :], ACT.Relu).then_inc(e_h, 1)
                m = s.back(4)
                if m.exists(EB):
                    act.wait_ge(e_m, m.n + 1)
                    if m.back(R).exists(EB):
                        act.wait_ge(s_mst[m.slot % R], m.use(R) * 16)
                    nc.scalar.activation(msg[:, m.slot % R, :, 0:D],
                                         ps_m[m.slot % 2][:, :].rearrange("p (g d) -> p g d", g=G),
                                         ACT.Copy).then_inc(e_msg, 1)
                z = s.back(3)
                if z.exists(EB):
                    act.wait_ge(e_z, z.n + 1)
                    if z.back(2).exists(EB):
                        act.wait_ge(e_m, z.back(2).n + 1)
                    nc.scalar.activation(tT[:, z.slot % 2, :], ps_z[z.slot % 2][:, :], ACT.Relu, bias=b1_col[:, 0:1])\
                      .then_inc(e_t, 1)

            run_blocks(act, EB, 4, edge_step)
            act.wait_ge(x_fac, EB)

            def node_step(s):
                if s.exists(NB):
                    act.wait_ge(s_x[s.slot], (s.turn + 1) * 16)
                    if s.back(2).exists(NB):
                        act.wait_ge(n_tr, s.back(2).n + 1)
                    else:
                        act.wait_ge(e_tr, EB)
                    for g in range(G):
                        last = normalise(xn[:, s.slot % 2, g, :], xb[:, s.slot, g, :], x_rstd[:, bass.ds(s.n * G + g, 1)],
                                         x_shift[:, bass.ds(s.n * G + g, 1)])
                    last.then_inc(n_norm, 1)
                h = s.back(1)
                if h.exists(NB):
                    act.wait_ge(n_tr, h.n + 1)
                    if h.back(2).exists(NB):
                        act.wait_ge(n_u, h.back(2).n + 1)
                    else:
                        act.wait_ge(e_z, EB)
                    nc.scalar.activation(hT[:, h.slot % 2, :], ps_t[h.slot % 2][:, :], ACT.Relu).then_inc(n_h, 1)
                u = s.back(2)
                if u.exists(NB):
                    act.wait_ge(n_u, u.n + 1)
                    if u.back(H).exists(NB):
                        act.wait_ge(n_y, u.back(H).n + 1)
                    nc.scalar.activation(r[:, u.slot % H, :, :].rearrange("p g d -> p (g d)"), ps_m[u.slot % 2][:, :],
                                         ACT.Relu).then_inc(n_r, 1)
                f = s.back(3)
                if f.exists(NB):
                    act.wait_ge(n_mom2, f.n + 1)
                    if f.back(R).exists(NB):
                        act.wait_ge(n_rstd2, f.back(R).n + 1)
                    standard_deviation(std2[:, f.slot % R, :], moments2[:, f.slot % R, :, 1]).then_inc(n_std2, 1)
                o = s.back(4)
                if o.exists(NB):
                    act.wait_ge(n_fac2, o.n + 1)
                    for g in range(DVE_TILES, G):
                        last = normalise(r[:, o.slot % H, g, :], r[:, o.slot % H, g, :], rstd2[:, o.slot % R, g:g + 1],
                                         shift2[:, o.slot % R, g:g + 1])
                    last.then_inc(n_ln[1], 1)

            run_blocks(act, NB, 4, node_step)

        @block.vector
        def _(dve):
            chain = [0]

            def link(ins):
                chain[0] += 1
                ins.then_inc(s_set, 1)
                dve.wait_ge(s_set, chain[0])

            def three_parts(parts, bias):
                link(nc.vector.tensor_copy(bias_hi[:, :], bias[:, :]))
                nc.vector.tensor_copy(parts[0:32, :], bias_hi[0:32, :])
                link(nc.vector.tensor_tensor(bias[:, :], bias[:, :], bias_hi[:, :], ALU.subtract))
                link(nc.vector.tensor_copy(bias_hi[:, :], bias[:, :]))
                nc.vector.tensor_copy(parts[32:64, :], bias_hi[32:64, :])
                link(nc.vector.tensor_tensor(bias[:, :], bias[:, :], bias_hi[:, :], ALU.subtract))
                nc.vector.tensor_copy(parts[64:96, :], bias[64:96, :])
                link(nc.vector.tensor_copy(parts[96:128, :], bias[96:128, :]))

            nc.vector.memset(msg[:, :, :, DST:], 0.0)
            link(nc.vector.memset(ones[:, :], 1.0))
            dve.wait_ge(s_types, 16)
            for k in range(TYPES):
                last = nc.vector.tensor_scalar(type_hot[:, k, :], type_sb[:, :], float(k), None, ALU.is_equal)
            last.then_inc(s_thot, 1)
            dve.wait_ge(s_ttr, 1)
            for k in range(TYPES):
                last = nc.vector.tensor_copy(type_turned[:, k, :], ps_z[k][0:SEG, :])
            last.then_inc(s_tcp, 1)
            dve.wait_ge(s_lists, 32)
            nc.vector.tensor_scalar(q_int[:, 0, :], dst_sb[:, :], PAIR_BITS + QL_BITS, None, ALU.arith_shift_right)
            nc.vector.tensor_scalar(q_int[:, 1, :], dst_sb[:, :], PAIR_BITS, QL - 1, ALU.arith_shift_right,
                                    ALU.bitwise_and)
            nc.vector.tensor_copy(dst_f[:, :], dst_sb[:, :])
            link(nc.vector.tensor_copy(next_f[:, :], next_sb[:, :]))
            nc.vector.tensor_copy(q_f[:, :, :], q_int[:, :, :])
            link(nc.vector.tensor_tensor(next_f[:, :], next_f[:, :], dst_f[:, :], ALU.is_lt))
            nc.vector.tensor_reduce(falls[:, 0:1], next_f[:, :], axis=AX.X, op=ALU.add)
            nc.vector.tensor_reduce(falls[:, 1:2], next_f[:, :], axis=AX.X, op=ALU.add).then_inc(s_falls, 1)
            dve.wait_ge(s_w, 160)
            dve.wait_ge(s_cst, 16)
            nc.vector.tensor_copy(pick_rows[:, :], cst[:, C_ROWS:C_ROWS + P])
            three_parts(b2_parts, b2_bc)
            three_parts(bs_parts, bs_bc)
            dve.sem_inc(s_bias, 1)

            def edge_step(s):
                if s.exists(EB):
                    dve.wait_ge(s_gather[s.slot % H], (s.use(H) + 1) * (16 * G))
                    for g in range(G):
                        last = nc.vector.bn_stats(stats[:, s.slot % 2, g, :], xg[:, s.slot % H, g, :])
                    last.then_inc(e_stats, 1)
                n = s.back(1)
                if n.exists(EB):
                    if n.back(2).exists(EB):
                        dve.wait_ge(e_norm, n.back(2).n + 1)
                    dve.wait_ge(e_std, n.n + 1)
                    nc.vector.reciprocal(rstd[:, n.slot % 2, :], std[:, n.slot % R, :]).then_inc(e_rinv, 1)
                    dve.wait_ge(e_rinv, n.n + 1)
                    nc.vector.scalar_tensor_tensor(shift[:, n.slot % 2, :], moments[:, n.slot % R, :, 0], -1.0,
                                                   rstd[:, n.slot % 2, :], ALU.mult, ALU.mult).then_inc(e_rstd, 1)
                elif s.exists(EB):
                    wait_ahead(dve, e_stats, s.n + 1)
                if s.exists(EB):
                    for g in range(G):
                        last = nc.vector.bn_aggr(moments[:, s.slot % R, g, :], stats[:, s.slot % 2, g, :])
                    last.then_inc(e_mom, 1)
                if s.exists(EB):
                    for i in range(2):
                        slot = (2 * s.slot + i) % U
                        dve.wait_ge(s_xa[slot], (s.turn * 2 + ((2 * s.slot + i) // U + 1)) * 16)
                        for g in range(G):
                            last = nc.vector.bn_stats(x_stats[:, s.slot % 2, i * G + g, :], xb[:, slot, g, :])
                    last.then_inc(x_st, 1)
                k = s.back(2)
                if k.exists(EB):
                    dve.wait_ge(x_sd, k.n + 1)
                    nc.vector.reciprocal(x_rstd[:, bass.ds(k.n * 2 * G, 2 * G)], x_std[:, k.slot % 2, :]).then_inc(x_inv, 1)
                if s.exists(EB):
                    if s.back(2).exists(EB):
                        dve.wait_ge(e_hist, s.back(2).n + 1)
                    for hot, i, n_ in ((hot_h, 0, QH), (hot_l, 1, QL)):
                        last = nc.vector.tensor_tensor(
                            hot[:, s.slot % 2, :, :], q_f[:, i, bass.ds(s.n * G, G)].unsqueeze(2).to_broadcast([P, G, n_]),
                            cst[:, C_QL:C_QL + n_].unsqueeze(1).to_broadcast([P, G, n_]), ALU.is_equal)
                    last.then_inc(e_hot, 1)
                m = s.back(4)
                if m.exists(EB):
                    if m.back(R).exists(EB):
                        dve.wait_ge(s_mst[m.slot % R], m.use(R) * 16)
                    nc.vector.tensor_copy(msg[:, m.slot % R, :, DST], dst_f[:, bass.ds(m.n * G, G)]).then_inc(e_dst, 1)
                if k.exists(EB):
                    dve.wait_ge(x_inv, k.n + 1)
                    nc.vector.scalar_tensor_tensor(x_shift[:, bass.ds(k.n * 2 * G, 2 * G)],
                                                   x_moments[:, k.slot % R, :, 0], -1.0,
                                                   x_rstd[:, bass.ds(k.n * 2 * G, 2 * G)], ALU.mult, ALU.mult)\
                      .then_inc(x_fac, 1)
                elif s.exists(EB):
                    wait_ahead(dve, x_st, s.n + 1)
                if s.exists(EB):
                    for g in range(2 * G):
                        last = nc.vector.bn_aggr(x_moments[:, s.slot % R, g, :], x_stats[:, s.slot % 2, g, :])
                    last.then_inc(x_mo, 1)

            run_blocks(dve, EB, 4, edge_step)

            dve.wait_ge(e_hist, EB)
            nc.vector.tensor_tensor(counts[:, :], ps_h[:, :], cst[0:G * QH, C_DIAG:C_DIAG + G * QL], ALU.mult)\
              .then_inc(s_folded, 1)
            dve.wait_ge(s_hist, 2)
            nc.vector.tensor_reduce(count[:, :], ps_q[:, 0:G * QL].rearrange("a (t b) -> a b t", t=G), axis=AX.X,
                                    op=ALU.add)
            link(nc.vector.tensor_scalar(is_sorted[:, :], ps_q[:, G * QL:G * QL + 2], 1.0, None, ALU.is_equal))
            link(nc.vector.tensor_tensor_scan(upto[:, :], ones[0:QH, 0:QL], count[:, :], 0.0, ALU.mult, ALU.add))
            nc.vector.tensor_copy(total[:, :], upto[:, QL - 1:QL].to_broadcast([QH, 2])).then_inc(s_tot, 1)
            dve.wait_ge(s_off, 1)
            link(nc.vector.tensor_copy(offset[:, :], ps_q[:, G * QL + 2:G * QL + 4]))
            link(nc.vector.tensor_tensor(upto[:, :], upto[:, :], count[:, :], ALU.subtract))
            nc.vector.tensor_scalar(tab_f[:, 0, :], upto[:, :], offset[:, 0:1], is_sorted[:, 0:1], ALU.add, ALU.mult)
            link(nc.vector.tensor_scalar(total[:, :], is_sorted[:, :], -float(EP), float(EP), ALU.mult, ALU.add))
            link(nc.vector.tensor_scalar(tab_f[:, 1, :], count[:, :], total[:, 0:1], float(P - 1), ALU.max, ALU.add))
            link(nc.vector.tensor_copy(tab_i[:, :, :], tab_f[:, :, :]))
            link(nc.vector.tensor_scalar(tab_i[:, 1, :], tab_i[:, 1, :], 8, PACK, ALU.arith_shift_right,
                                         ALU.logical_shift_left))
            nc.vector.tensor_tensor(tab_packed[:, :], tab_i[:, 1, :], tab_i[:, 0, :], ALU.bitwise_or).then_inc(s_tabi, 1)

            dve.wait_ge(s_tab, 16)
            doubles = running_counts(dve, "dve")

            def select_extra(s, q, to, window):
                return nc.vector.tensor_scalar(to, slot_of, window[:, DST:DST + 1],
                                               cst[:, bass.ds(s.n * 2 + C_BASE + q, 1)], ALU.subtract, ALU.is_equal)

            def node_step(s):
                f = s.back(3)
                if f.exists(NB):
                    dve.wait_ge(n_r, f.n + 1)
                    for g in range(G):
                        last = nc.vector.bn_stats(stats2[:, f.slot % 2, g, :], r[:, f.slot % H, g, :])
                    last.then_inc(n_stats2, 1)
                o = s.back(4)
                if o.exists(NB):
                    dve.wait_ge(n_std2, o.n + 1)
                    if o.back(R).exists(NB):
                        dve.wait_ge(n_gam, o.back(R).n + 1)
                    nc.vector.reciprocal(rstd2[:, o.slot % R, :], std2[:, o.slot % R, :]).then_inc(n_rstd2, 1)
                w = s.back(1)
                if w.exists(NB):
                    dve.wait_ge(n_rel, w.n + 1)
                    if w.back(2).exists(NB):
                        dve.wait_ge(n_u, w.back(2).n + 1)
                    for q in range(2):
                        last = nc.vector.tensor_scalar(sel[:, w.slot % 2, q, :], slot_of, rel[:, w.slot % R, q:q + 1],
                                                       None, ALU.is_equal)
                    last.then_inc(n_sel, 1)
                if o.exists(NB):
                    dve.wait_ge(n_rstd2, o.n + 1)
                    nc.vector.scalar_tensor_tensor(shift2[:, o.slot % R, :], moments2[:, o.slot % R, :, 0], -1.0,
                                                   rstd2[:, o.slot % R, :], ALU.mult, ALU.mult).then_inc(n_fac2, 1)
                elif f.exists(NB):
                    wait_ahead(dve, n_stats2, f.n + 1)
                if f.exists(NB):
                    for g in range(G):
                        last = nc.vector.bn_aggr(moments2[:, f.slot % R, g, :], stats2[:, f.slot % 2, g, :])
                    last.then_inc(n_mom2, 1)
                if o.exists(NB):
                    dve.wait_ge(n_fac2, o.n + 1)
                    for g in range(DVE_TILES):
                        last = nc.vector.tensor_scalar(r[:, o.slot % H, g, :], r[:, o.slot % H, g, :],
                                                       rstd2[:, o.slot % R, g:g + 1], shift2[:, o.slot % R, g:g + 1],
                                                       ALU.mult, ALU.add)
                    last.then_inc(n_ln[0], 1)
                if w.exists(NB):
                    entries = load_table(dve, w)
                y_ = s.back(6)
                if y_.exists(NB):
                    dve.wait_ge(n_gam, y_.n + 1)
                    dve.wait_ge(n_xb, y_.n + 1)
                    if y_.back(R).exists(NB):
                        dve.wait_ge(s_out[y_.slot % R], y_.use(R) * 16)
                    nc.vector.tensor_tensor(y[:, y_.slot % R, :, :], r[:, y_.slot % H, :, :], xb[:, y_.slot, :, :], ALU.add)\
                      .then_inc(n_y, 1)
                if w.exists(NB):
                    def select(q, es, c):
                        done = dve.snap(doubles[es])
                        dve.wait_ge(s_winx[es], (done + 1) * 16)
                        dve.wait_ge(x_used[es], done + 1)
                        for i in range(2):
                            last = select_extra(w, q, sel_x[:, es, i, :], win_x[:, es, i, :])
                        last.then_inc(x_sel[es], 1)

                    for_extras(dve, w, entries, doubles, select)

            run_blocks(dve, NB, 6, node_step)

        @block.tensor
        def _(pe):
            pe.wait_ge(s_cst, 16)
            pe.wait_ge(s_thot, 1)
            for k in range(TYPES):
                for c in range(G):
                    last = nc.tensor.transpose(ps_z[k][0:SEG, c * P:(c + 1) * P], type_hot[:, k, c * SEG:(c + 1) * SEG],
                                               ident)
            last.then_inc(s_ttr, 1)
            pe.wait_ge(s_falls, 1)
            nc.tensor.matmul(ps_q[:, G * QL:G * QL + 2], ones[:, 0:QH], falls[:, :], start=True, stop=True)\
              .then_inc(s_hist, 1)
            pe.wait_ge(s_w, 160)
            pe.wait_ge(s_bias, 1)

            def edge_step(s):
                if s.exists(EB):
                    pe.wait_ge(e_norm, s.n + 1)
                    if s.back(2).exists(EB):
                        pe.wait_ge(e_h, s.back(2).n + 1)
                    for g in range(G):
                        last = nc.tensor.transpose(ps_t[s.slot % 2][:, g * P:(g + 1) * P], xn[:, s.slot % 2, g, :], ident)
                    last.then_inc(e_tr, 1)
                z = s.back(1)
                if z.exists(EB):
                    pe.wait_ge(s_ez[z.slot % R], (z.use(R) + 1) * 32)
                    if z.back(2).exists(EB):
                        pe.wait_ge(e_t, z.back(2).n + 1)
                    nc.tensor.matmul(ps_z[z.slot % 2][:, :], w1_e[:, :], ez[:, z.slot % R, :], start=True, stop=False)
                    pe.wait_ge(e_h, z.n + 1)
                    nc.tensor.matmul(ps_z[z.slot % 2][:, :], w1_x[:, :], hT[:, z.slot % 2, :], start=False, stop=True)\
                      .then_inc(e_z, 1)
                if s.exists(EB):
                    pe.wait_ge(e_hot, s.n + 1)
                    nc.tensor.matmul(ps_h[:, :], hot_h[:, s.slot % 2, :, :].rearrange("p t a -> p (t a)"),
                                     hot_l[:, s.slot % 2, :, :].rearrange("p t a -> p (t a)"),
                                     start=s.is_block(0), stop=s.is_block(EB - 1)).then_inc(e_hist, 1)
                m = s.back(2)
                if m.exists(EB):
                    if m.back(2).exists(EB):
                        pe.wait_ge(e_msg, m.back(2).n + 1)
                    nc.tensor.matmul(ps_m[m.slot % 2][:, :], pick_rows[:, :], b2_parts[:, :], start=True, stop=False)
                    pe.wait_ge(e_t, m.n + 1)
                    for g in range(G):
                        last = nc.tensor.matmul(ps_m[m.slot % 2][:, g * D:(g + 1) * D],
                                                tT[:, m.slot % 2, g * P:(g + 1) * P], w2_sb[:, :], start=False,
                                                stop=(g == G - 1))
                    last.then_inc(e_m, 1)

            run_blocks(pe, EB, 2, edge_step)

            pe.wait_ge(s_folded, 1)
            nc.tensor.matmul(ps_q[:, 0:G * QL], cst[0:G * QH, C_FOLD:C_FOLD + QH], counts[:, :], start=True, stop=True)\
              .then_inc(s_hist, 1)
            pe.wait_ge(s_tot, 1)
            nc.tensor.matmul(ps_q[:, G * QL + 2:G * QL + 4], tri[0:QH, 0:QH], total[:, :], start=True, stop=True).then_inc(s_off, 1)

            doubles = running_counts(pe, "pe")
            for i in range(EXTRA_SLOTS):
                pe.sem_inc(x_used[i], 1)

            def node_step(s):
                if s.exists(NB):
                    pe.wait_ge(n_norm, s.n + 1)
                    if s.back(2).exists(NB):
                        pe.wait_ge(n_h, s.back(2).n + 1)
                    else:
                        pe.wait_ge(e_h, EB)
                    for g in range(G):
                        last = nc.tensor.transpose(ps_t[s.slot % 2][:, g * P:(g + 1) * P], xn[:, s.slot % 2, g, :], ident)
                    last.then_inc(n_tr, 1)
                u = s.back(1)
                if u.exists(NB):
                    if u.is_block(0):
                        pe.wait_ge(s_tab, 16)
                    entries = load_table(pe, u)
                    ps_u = ps_m[u.slot % 2]
                    if u.back(2).exists(NB):
                        pe.wait_ge(n_r, u.back(2).n + 1)
                    else:
                        pe.wait_ge(e_msg, EB)
                    nc.tensor.matmul(ps_u[:, :], pick_rows[:, :], bs_parts[:, :], start=True, stop=False)
                    pe.wait_ge(n_h, u.n + 1)
                    for g in range(G):
                        nc.tensor.matmul(ps_u[:, g * D:(g + 1) * D], hT[:, u.slot % 2, g * P:(g + 1) * P], ws_sb[:, :],
                                         start=False, stop=False)
                    def multiply(q, es, c):
                        pe.wait_ge(x_sel[es], pe.snap(doubles[es]) + 1)
                        for w in range(2):
                            for k in range(2):
                                g = 2 * q + k
                                last = nc.tensor.matmul(ps_u[:, g * D:(g + 1) * D],
                                                        sel_x[:, es, w, k * P:(k + 1) * P], win_x[:, es, w, 0:D],
                                                        start=False, stop=False)
                        last.then_inc(x_used[es], 1)

                    for_extras(pe, u, entries, doubles, multiply)
                    pe.wait_ge(n_sel, u.n + 1)
                    for q in range(2):
                        for k in range(2):
                            g = 2 * q + k
                            last = nc.tensor.matmul(ps_u[:, g * D:(g + 1) * D], sel[:, u.slot % 2, q, k * P:(k + 1) * P],
                                                    win[:, u.slot % R, q, 0:D], start=False, stop=(g == G - 1))
                    last.then_inc(n_u, 1)

            run_blocks(pe, NB, 1, node_step)


def kernel(x, src, dst, edge_attr_16, edge_type_2, L0_gnn_W1, L0_gnn_b1, L0_gnn_W2, L0_gnn_b2, L0_gnn_Ws, L0_gnn_bs,
           L0_gnn_gamma, L0_gnn_beta):
    import concourse.bacc as bacc
    from concourse.bass_utils import run_bass_kernel_spmd

    def padded(a, rows, fill=0):
        a = np.asarray(a)
        whole = np.full((rows,) + a.shape[1:], fill, a.dtype)
        whole[:len(a)] = a
        return whole

    dst_all = padded(dst, EP + 1, -1)
    feats = padded(edge_attr_16, EP).reshape(P, EB, G, EF).transpose(1, 3, 2, 0).reshape(EB, EF, BLK)

    consts = np.zeros((P, C_END), np.float32)
    consts[:, C_ID:C_ID + P] = np.eye(P)
    consts[:, C_SLOT:C_SLOT + PAIR] = np.arange(PAIR).reshape(P, 2).T.reshape(1, PAIR)
    consts[:, C_BASE:C_BASE + PAIRS] = -np.arange(0, NP, PAIR)
    consts[:, C_QL:C_QL + QL] = np.arange(QL)
    consts[:, C_TRI:C_TRI + P] = np.triu(np.ones((P, P)), 1)
    consts[[0, 32, 64], C_ROWS:C_ROWS + P] = 1.0
    consts[:, C_EPS] = EPS
    consts[:G * QH, C_DIAG:C_DIAG + G * QL] = np.kron(np.eye(G), np.ones((QH, QL)))
    consts[:G * QH, C_FOLD:C_FOLD + QH] = np.tile(np.eye(QH), (G, 1))

    arrays = {
        "x": padded(x, NP), "src": padded(src, EP).reshape(P, ET), "dst": dst_all[:EP].reshape(P, ET),
        "dst_next": dst_all[1:].reshape(P, ET), "types": padded(edge_type_2, EP).reshape(P, ET), "feats": feats,
        "w1": L0_gnn_W1, "b1": np.asarray(L0_gnn_b1).reshape(D, 1), "w2": L0_gnn_W2, "b2": np.tile(np.asarray(L0_gnn_b2), G), "ws": L0_gnn_Ws,
        "bs": np.tile(np.asarray(L0_gnn_bs), G), "gamma": L0_gnn_gamma, "beta": L0_gnn_beta, "consts": consts,
    }
    arrays = {f"in_{k}": np.ascontiguousarray(a) for k, a in arrays.items()}
    nc = bacc.Bacc("TRN2", target_bir_lowering=False, num_devices=1)
    args = [nc.dram_tensor(k, a.shape, mybir.dt.from_np(a.dtype), kind="ExternalInput").ap() for k, a in arrays.items()]
    out = nc.dram_tensor("out", (NP, D), mybir.dt.float32, kind="ExternalOutput").ap()
    build(nc, *args, out)
    result = run_bass_kernel_spmd(nc, [arrays], core_ids=[0])
    return result.results[0]["out"][:N]
```

```python
from contextlib import ExitStack

import numpy as np

import concourse.bass as bass
from concourse import mybir

P = 128
D = 128
N = 100000
E = 50000
EF = 16
TYPES = 2
G = 4
BLK = G * P
EB = -(-E // BLK)
ET = EB * G
EP = EB * BLK
NB = -(-N // BLK)
NP = NB * BLK
PAIR = 2 * P
PAIRS = NP // PAIR
ROW = D + 4
DST = D
QL = 32
QH = -(-PAIRS // QL)
PAIR_BITS, QL_BITS, WINDOW_BITS = 8, 5, 7
EPS = 1e-5
U = 12
H = 6
R = 4
DVE_TILES = 3
Y_TILES = 3
LATER = 8
RUN = 4
SECONDS = 2
EXTRA_SLOTS = LATER + SECONDS
T = 3 * G
GROUP = 4

C_ID = 0
C_SLOT = C_ID + P
C_BASE = C_SLOT + PAIR
C_QL = C_BASE + PAIRS
C_TRI = C_QL + QL
C_ROWS = C_TRI + P
C_EPS = C_ROWS + P
C_DIAG = C_EPS + 1
C_FOLD = C_DIAG + G * QL
C_END = C_FOLD + QH

SEG = ET // G

assert NB % U >= 3 and U == 2 * H and U % GROUP == 0 and NB + GROUP < QH * QL // 2
assert NB == 2 * EB and SEG <= P and G * QH <= P
assert 1 << PAIR_BITS == PAIR and 1 << WINDOW_BITS == P and 1 << QL_BITS == QL and QH <= P


class Step:

    def __init__(self, turn, slot):
        self.turn, self.slot = turn, slot

    @property
    def n(self):
        return self.turn * U + self.slot

    def back(self, k):
        return Step(self.turn + (self.slot - k) // U, (self.slot - k) % U)

    def use(self, ring):
        return self.turn * (U // ring) + self.slot // ring

    def is_block(self, n):
        return isinstance(self.turn, int) and self.n == n

    def exists(self, total):
        return not isinstance(self.turn, int) or 0 <= self.n < total


def run_blocks(eng, total, lag, step):
    turns = total // U
    for n in range(U):
        step(Step(n // U, n % U))
    with eng.Fori(1, turns) as turn:
        for slot in range(U):
            step(Step(turn, slot))
    for n in range(turns * U, total + lag):
        step(Step(n // U, n % U))


def build(nc, x, src, dst, dst_next, types, ef_rows, w1, b1, w2, b2, ws, bs, gamma, beta, consts, out):
    f32, bf16, i32 = mybir.dt.float32, mybir.dt.bfloat16, mybir.dt.int32
    ALU, ACT = mybir.AluOpType, mybir.ActivationFunctionType
    AX = mybir.AxisListType

    messages = nc.dram_tensor("messages", (EP + 2 * P, ROW), f32, kind="Internal").ap()
    hot_types = nc.dram_tensor("hot_types", (TYPES, ET, P), f32, kind="Internal").ap()
    msg_store = messages[0:EP, :].rearrange("(p b g) r -> b p g r", p=P, g=G)
    x_rows = x.rearrange("(b q p k) d -> b p q (k d)", q=2, p=P, k=2)
    out_rows = out.rearrange("(b q p k) d -> b p q (k d)", q=2, p=P, k=2)

    ctx = ExitStack()
    with ctx:
        def sb(name, shape, dt=f32):
            return ctx.enter_context(nc.sbuf_tensor(name, shape, dt))

        def pb(name, shape, dt=f32):
            return ctx.enter_context(nc.psum_tensor(name, shape, dt))

        def sem(name):
            return ctx.enter_context(nc.semaphore(name))

        cst = sb("cst", [P, C_END])
        ident = cst[:, C_ID:C_ID + P]
        slot_of = cst[:, C_SLOT:C_SLOT + PAIR]
        tri = cst[:, C_TRI:C_TRI + P]
        w1_x = sb("w1_x", [D, D])
        w1_e = sb("w1_e", [TYPES + EF, D])
        w2_sb = sb("w2_sb", [D, D])
        ws_sb = sb("ws_sb", [D, D])
        b1_col = sb("b1_col", [D, 1])
        b2_bc = sb("b2_bc", [P, BLK])
        b2_parts = sb("b2_parts", [P, BLK], bf16)
        bs_bc = sb("bs_bc", [P, BLK])
        gamma_bc = sb("gamma_bc", [P, D])
        beta_bc = sb("beta_bc", [P, D])
        pick_rows = sb("pick_rows", [P, P], bf16)
        bs_parts = sb("bs_parts", [P, BLK], bf16)
        bias_hi = sb("bias_hi", [P, BLK], bf16)
        dst_sb = sb("dst_sb", [P, ET], i32)
        next_sb = sb("next_sb", [P, ET], i32)
        dst_f = sb("dst_f", [P, ET])
        next_f = sb("next_f", [P, ET])
        q_int = sb("q_int", [P, 2, ET], i32)
        q_f = sb("q_f", [P, 2, ET])
        hot_h = sb("hot_h", [P, R, G, QH], bf16)
        hot_l = sb("hot_l", [P, R, G, QL], bf16)
        type_sb = sb("type_sb", [P, ET], i32)
        type_hot = sb("type_hot", [P, TYPES, ET])
        type_turned = sb("type_turned", [SEG, TYPES, G * P])
        counts = sb("counts", [G * QH, G * QL])
        falls = sb("falls", [P, 2])
        ones = sb("ones", [P, P])
        count = sb("count", [QH, QL])
        upto = sb("upto", [QH, QL])
        total = sb("total", [QH, 2])
        offset = sb("offset", [QH, 2])
        is_sorted = sb("is_sorted", [QH, 2])
        tab_f = sb("tab_f", [QH, 2, QL])
        tab_i = sb("tab_i", [QH, 2, QL], i32)
        table = sb("table", [1, 2, 2 + QH * QL], i32)
        pad_rows = sb("pad_rows", [P, 2, ROW])
        xg = sb("xg", [P, H, G, D])
        idx = sb("idx", [P, H, G], i32)
        ez = sb("ez", [TYPES + EF, H, BLK])
        msg = sb("msg", [P, R, G, ROW])
        stats = sb("stats", [P, 2, T, 6])
        mean_sum = sb("mean_sum", [P, 2, T])
        mean_gap = sb("mean_gap", [P, 2, T])
        spread = sb("spread", [P, 2, T])
        std = sb("std", [P, R, T])
        rstd = sb("rstd", [P, EB * T])
        shift = sb("shift", [P, EB * T])
        xn = sb("xn", [P, 2, G, D])
        hT = sb("hT", [D, 2, BLK])
        tT = sb("tT", [D, 2, BLK])
        xb = sb("xb", [P, U, G, D])
        win = sb("win", [P, R, 2, 2, ROW])
        rel = sb("rel", [P, R, 2])
        sel = sb("sel", [P, 2, 2, PAIR])
        win_x = sb("win_x", [P, LATER, 2, ROW])
        sel_x = sb("sel_x", [P, EXTRA_SLOTS, 2, PAIR])
        r = sb("r", [P, H, G, D])
        stats2 = sb("stats2", [P, 2, G, 6])
        moments2 = sb("moments2", [P, R, G, 2])
        std2 = sb("std2", [P, R, G])
        rstd2 = sb("rstd2", [P, R, G])
        shift2 = sb("shift2", [P, R, G])
        y = sb("y", [P, R, G, D])

        ps_t = [pb(f"ps_t{i}", [D, BLK]) for i in range(2)]
        ps_z = [pb(f"ps_z{i}", [D, BLK]) for i in range(2)]
        ps_m = [pb(f"ps_m{i}", [P, BLK]) for i in range(2)]
        ps_q = pb("ps_q", [QH, BLK])
        ps_h = pb("ps_h", [G * QH, G * QL])

        s_idx = [sem(f"src_loaded{i}") for i in range(H)]
        s_lists = sem("dst_loaded")
        s_cst = sem("consts_loaded")
        s_w = sem("weights_loaded")
        s_gather = [sem(f"gathered{i}") for i in range(H)]
        s_ez = [sem(f"edge_feats_loaded{i}") for i in range(H)]
        s_types = sem("types_list_loaded")
        s_turned = sem("types_turned_stored")
        s_xa = [sem(f"x_loaded_for_stats{i}") for i in range(U)]
        s_mst = [sem(f"messages_stored{i}") for i in range(R)]
        s_pad = sem("pad_rows_stored")
        s_tab = sem("table_ready")
        s_x = [sem(f"x_loaded{i}") for i in range(U)]
        s_win = [sem(f"windows_loaded{i}") for i in range(R)]
        s_winx = [sem(f"later_windows_loaded{i}") for i in range(LATER)]
        s_out = [sem(f"out_stored{i}") for i in range(R)]
        s_set = sem("setup_chain")
        s_passed = sem("waits_passed")
        s_fill = sem("fills_done")
        s_bias = sem("b2_parts_ready")
        s_bs = sem("bs_parts_ready")
        s_falls = sem("falls_counted_by_row")
        e_hot = sem("pair_one_hots")
        e_hist = sem("histogram_added")
        s_thot = sem("types_hot")
        s_ttr = sem("types_transposed")
        s_tcp = sem("types_turned")
        s_hist = sem("histogram_ready")
        s_folded = sem("histogram_masked")
        s_tot = sem("totals_ready")
        s_off = sem("offsets_ready")
        s_tabi = sem("table_computed")
        e_stats = sem("stats")
        e_sums = sem("sums_of_stats")
        e_gap = sem("gaps_squared")
        e_mom = sem("moments")
        e_std = sem("std")
        e_inv = sem("inverse_std")
        e_rstd = sem("rstd_and_shift")
        e_norm = sem("edge_normed")
        e_tr = sem("edge_transposed")
        e_h = sem("edge_hT")
        e_z = sem("edge_z")
        e_t = sem("edge_tT")
        e_m = sem("edge_m")
        e_msg = sem("edge_msg")
        e_dst = sem("edge_msg_dst")
        n_norm = sem("node_normed")
        n_tr = sem("node_transposed")
        n_h = sem("node_hT")
        n_sel = sem("node_sel")
        n_xb = sem("node_x_beta")
        n_u = sem("node_u")
        n_r = sem("node_r")
        n_stats2 = sem("node_stats2")
        n_mom2 = sem("node_moments2")
        n_std2 = sem("node_std2")
        n_rstd2 = sem("node_rstd2")
        n_fac2 = sem("node_rstd2_shift2")
        n_ln = [sem(f"node_normalised{i}") for i in range(2)]
        n_gam = sem("node_times_gamma")
        n_rel = sem("node_rel")
        n_y = [sem(f"node_y{i}") for i in range(2)]
        x_sel = [sem(f"extra_sel{i}") for i in range(EXTRA_SLOTS)]
        x_used = [sem(f"later_windows_used{i}") for i in range(LATER)]

        def for_later(eng, s, counts, turns, later):
            def in_turn(q, c, i):
                es = (4 * (s.slot % 2) + 2 * q + i) % LATER
                later(q, es, c + 2 * i)
                eng.reg_add(turns[es], turns[es], 1)
                if i + 1 < RUN:
                    with eng.If(c + 2 * (i + 1) < counts[q]):
                        in_turn(q, c, i + 1)

            with eng.If((counts[0] | counts[1]) > 1):
                for q in range(2):
                    with eng.If(counts[q] > 1):
                        with eng.Fori(1, counts[q], 2 * RUN) as c:
                            in_turn(q, c, 0)

        def for_extras(eng, s, counts, turns, second, later):
            with eng.If((counts[0] | counts[1]) > 0):
                es = LATER + s.slot % SECONDS
                second(es)
                eng.reg_add(turns[es], turns[es], 1)
                for_later(eng, s, counts, turns, later)

        def running_counts(eng, name):
            turns = [eng.alloc_register(f"{name}_turns{i}") for i in range(EXTRA_SLOTS)]
            for reg in turns:
                eng.reg_mov(reg, 0)
            return turns

        def wait_ahead(eng, semaphore, value):
            eng.wait_ge(semaphore, value)
            eng.sem_inc(s_passed, 1)

        def table_reader(eng, lag, kinds):
            held = {}

            def read(s):
                if s.slot % GROUP == 0:
                    for kind in kinds:
                        row = table[0:1, kind, bass.ds((s.n + (1 - lag)) * 2, 2 * GROUP)]
                        _, held[kind] = nc.values_load_multi_w_load_instructions(
                            row, engines=[eng.engine], min_val=0, max_val=EP,
                            skip_runtime_bounds_check_because="the table's entries are at most EP by its construction")
                at = 2 * (s.slot % GROUP)
                return [held[kind][at:at + 2] for kind in kinds]

            return read

        block = ctx.enter_context(nc.Block())

        @block.sync
        def _(sp):
            def load_src(s):
                sp.dma_start(idx[:, s.slot % H, :], src[:, bass.ds(s.n * G, G)]).then_inc(s_idx[s.slot % H], 16)

            for n in range(H):
                load_src(Step(0, n))
            sp.dma_start(type_sb[:, :], types).then_inc(s_types, 16)
            sp.dma_start(dst_sb[:, :], dst).then_inc(s_lists, 16)
            sp.dma_start(next_sb[:, :], dst_next).then_inc(s_lists, 16)
            sp.dma_start(cst[:, :], consts).then_inc(s_cst, 16)
            sp.dma_start(w1_x[:, :], w1[0:D, :]).then_inc(s_w, 16)
            sp.dma_start(w1_e[0:TYPES, :], w1[D + EF:D + EF + TYPES, :]).then_inc(s_w, 16)
            sp.dma_start(w1_e[TYPES:TYPES + EF, :], w1[D:D + EF, :]).then_inc(s_w, 16)
            sp.dma_start(w2_sb[:, :], w2).then_inc(s_w, 16)
            sp.dma_start(b1_col[:, :], b1).then_inc(s_w, 16)
            sp.dma_start(b2_bc[:, :], b2.partition_broadcast(P)).then_inc(s_w, 16)
            sp.dma_start(ws_sb[:, :], ws).then_inc(s_w, 16)
            sp.dma_start(bs_bc[:, :], bs.partition_broadcast(P)).then_inc(s_w, 16)
            sp.dma_start(gamma_bc[:, :], gamma.partition_broadcast(P)).then_inc(s_w, 16)
            sp.dma_start(beta_bc[:, :], beta.partition_broadcast(P)).then_inc(s_w, 16)

            def load_x(ring, slot, n):
                sp.dma_start(xb[:, slot, :, :].rearrange("p (q k) d -> p q (k d)", q=2),
                             x_rows[bass.ds(n, 1), :, :, :].rearrange("a p q f -> (a p) q f")).then_inc(ring[slot], 16)

            for n in range(2 * H):
                load_x(s_xa, n, n)

            sp.wait_ge(s_tcp, 1)
            for k in range(TYPES):
                sp.dma_start(hot_types[k].rearrange("(c t) p -> t c p", c=G),
                             type_turned[:, k, :].rearrange("t (c p) -> t c p", c=G)).then_inc(s_turned, 16)
            sp.wait_ge(s_turned, 16 * TYPES)

            sp.wait_ge(s_fill, 1)
            sp.dma_start(messages[EP:EP + 2 * P, :].rearrange("(p k) r -> p k r", k=2), pad_rows[:, :, :])\
              .then_inc(s_pad, 16)

            def edge_step(s):
                if s.exists(EB):
                    if s.back(H).exists(EB):
                        sp.wait_ge(e_stats, s.back(H).n + 1)
                        load_src(s)
                        sp.wait_ge(e_z, s.back(H).n + 1)
                    sp.dma_start(ez[0:TYPES, s.slot % H, :].rearrange("k (t p) -> k t p", t=G),
                                 hot_types[:, bass.ds(s.n * G, G), :]).then_inc(s_ez[s.slot % H], 16)
                    sp.dma_start(ez[TYPES:, s.slot % H, :], ef_rows[bass.ds(s.n, 1), :, :].rearrange("a t e -> (a t) e"))\
                      .then_inc(s_ez[s.slot % H], 16)
                    for i in range(2 if s.back(H).exists(EB) else 0):
                        load_x(s_xa, (2 * s.slot + i) % U, s.n * 2 + i)
                if s.is_block(EB + 1):
                    sp.wait_ge(e_stats, EB)
                    for n in range(3):
                        load_x(s_x, n, n)
                m = s.back(8)
                if m.exists(EB):
                    sp.wait_ge(e_msg, m.n + 1)
                    sp.wait_ge(e_dst, m.n + 1)
                    sp.dma_start(msg_store[bass.ds(m.n, 1), :, :, :].rearrange("a p g r -> (a p) g r"),
                                 msg[:, m.slot % R, :, :]).then_inc(s_mst[m.slot % R], 16)

            run_blocks(sp, EB, 8, edge_step)
            sp.wait_ge(s_tabi, 1)
            for kind in range(2):
                sp.dma_start(table[:, kind, 2:].rearrange("o (a b) -> o a b", a=QH), tab_i[:, kind, :])\
                  .then_inc(s_tab, 16)
            for n in range(3, R + 3):
                load_x(s_x, n, n)
            sp.wait_ge(s_tab, 32)
            sp.wait_ge(s_pad, 16)
            for i in range(R):
                sp.wait_ge(s_mst[i], 16 * len(range(i, EB, R)))

            turns = running_counts(sp, "sp")
            read_table = table_reader(sp, 0, (0, 1))

            def node_step(s):
                o = s.back(9)
                if o.exists(NB):
                    for y_ready in n_y:
                        sp.wait_ge(y_ready, o.n + 1)
                    sp.dma_start(out_rows[bass.ds(o.n, 1), :, :, :].rearrange("a p q f -> (a p) q f"),
                                 y[:, o.slot % R, :, :].rearrange("p (q k) d -> p q (k d)", q=2)).then_inc(s_out[o.slot % R], 16)
                if s.exists(NB) and s.back(R).exists(NB):
                    sp.wait_ge(n_u, s.back(R).n + 1)
                if o.exists(NB):
                    ahead = o.back(-U)
                    if ahead.exists(NB):
                        load_x(s_x, ahead.slot, ahead.n)
                if s.is_block(1):
                    for n in range(R + 3, U):
                        load_x(s_x, n, n)
                if s.exists(NB):
                    first, counts = read_table(s)
                    def load_later(q, es, c):
                        start = nc.s_assert_within(sp.snap(first[q] + P + c * P), 0, EP,
                                                   skip_runtime_bounds_check_because="the windows start before EP")
                        sp.wait_ge(x_used[es], sp.snap(turns[es]) + 1)
                        sp.dma_start(win_x[:, es, :, :], messages[bass.ds(start, 2 * P), :]
                                     .rearrange("(k p) r -> p k r", k=2)).then_inc(s_winx[es], 16)

                    def load_first(n):
                        for q in range(2):
                            sp.dma_start(win[:, s.slot % R, q, 0:n, :], messages[bass.ds(first[q], n * P), :]
                                         .rearrange("(k p) r -> p k r", k=n)).then_inc(s_win[s.slot % R], 16)

                    with sp.If((counts[0] | counts[1]) < 1):
                        load_first(1)
                    with sp.If((counts[0] | counts[1]) > 0):
                        load_first(2)
                        for_later(sp, s, counts, turns, load_later)

            run_blocks(sp, NB, 9, node_step)
            for i in range(R):
                sp.wait_ge(s_out[i], 16 * len(range(i, NB, R)))

        @block.gpsimd
        def _(pool):
            nc.gpsimd.memset(pad_rows[:, :, :], -1.0).then_inc(s_fill, 1)

            def edge_step(s):
                free = s.back(H)
                if free.exists(EB):
                    pool.wait_ge(e_norm, free.n + 1)
                wait_ahead(pool, s_idx[s.slot % H], (s.use(H) + 1) * 16)
                for g in range(G):
                    pool.indirect_dma_start(
                        out=xg[:, s.slot % H, g, :], out_offset=None, in_=x,
                        in_offset=bass.IndirectOffsetOnAxis(ap=idx[:, s.slot % H, g:g + 1], axis=0),
                    ).then_inc(s_gather[s.slot % H], 16)

            run_blocks(pool, EB, 0, edge_step)

            pool.wait_ge(s_w, 160)

            def node_step(s):
                if s.exists(NB):
                    pool.wait_ge(s_win[s.slot % R], (s.use(R) + 1) * 32)
                    if s.back(R).exists(NB):
                        pool.wait_ge(n_sel, s.back(R).n + 1)
                    nc.gpsimd.tensor_tensor(rel[:, s.slot % R, :], win[:, s.slot % R, :, 0, DST],
                                            cst[:, bass.ds(s.n * 2 + C_BASE, 2)], ALU.add).then_inc(n_rel, 1)
                y_ = s.back(6)
                if y_.exists(NB):
                    pool.wait_ge(n_gam, y_.n + 1)
                    if y_.back(R).exists(NB):
                        pool.wait_ge(s_out[y_.slot % R], y_.use(R) * 16)
                    nc.gpsimd.tensor_tensor(y[:, y_.slot % R, Y_TILES:, :], r[:, y_.slot % H, Y_TILES:, :],
                                            xb[:, y_.slot, Y_TILES:, :], ALU.add).then_inc(n_y[1], 1)
                b = s.back(1)
                if b.exists(NB):
                    pool.wait_ge(n_norm, b.n + 1)
                    nc.gpsimd.tensor_tensor(xb[:, b.slot, :, :], xb[:, b.slot, :, :],
                                            beta_bc[:, :].unsqueeze(1).to_broadcast([P, G, D]), ALU.add)\
                      .then_inc(n_xb, 1)
                o = s.back(5)
                if o.exists(NB):
                    for sem_ in n_ln:
                        pool.wait_ge(sem_, o.n + 1)
                    nc.gpsimd.tensor_tensor(r[:, o.slot % H, :, :], r[:, o.slot % H, :, :],
                                            gamma_bc[:, :].unsqueeze(1).to_broadcast([P, G, D]), ALU.mult)\
                      .then_inc(n_gam, 1)

            run_blocks(pool, NB, 6, node_step)

        @block.scalar
        def _(act):
            act.wait_ge(s_w, 160)
            act.wait_ge(s_cst, 16)

            def standard_deviation(to, of, scale=1.0):
                return nc.scalar.activation(to, of, ACT.Sqrt, bias=cst[:, C_EPS:C_EPS + 1], scale=scale)

            def normalise(to, of, scale, shift_):
                return nc.scalar.activation(to, of, ACT.Identity, bias=shift_, scale=scale)

            def edge_step(s):
                if s.exists(EB):
                    act.wait_ge(e_mom, s.n + 1)
                    if s.back(R).exists(EB):
                        act.wait_ge(e_inv, s.back(R).n + 1)
                    standard_deviation(std[:, s.slot % R, :], spread[:, s.slot % 2, :], 1.0 / D).then_inc(e_std, 1)
                n = s.back(1)
                if n.exists(EB):
                    act.wait_ge(e_rstd, n.n + 1)
                    if n.back(2).exists(EB):
                        act.wait_ge(e_tr, n.back(2).n + 1)
                    for g in range(G):
                        last = normalise(xn[:, n.slot % 2, g, :], xg[:, n.slot % H, g, :],
                                         rstd[:, bass.ds(n.n * T + g, 1)], shift[:, bass.ds(n.n * T + g, 1)])
                    last.then_inc(e_norm, 1)
                h = s.back(2)
                if h.exists(EB):
                    act.wait_ge(e_tr, h.n + 1)
                    if h.back(2).exists(EB):
                        act.wait_ge(e_z, h.back(2).n + 1)
                    nc.scalar.activation(hT[:, h.slot % 2, :], ps_t[h.slot % 2][:, :], ACT.Relu).then_inc(e_h, 1)
                m = s.back(4)
                if m.exists(EB):
                    act.wait_ge(e_m, m.n + 1)
                    if m.back(R).exists(EB):
                        act.wait_ge(s_mst[m.slot % R], m.use(R) * 16)
                    nc.scalar.activation(msg[:, m.slot % R, :, 0:D],
                                         ps_m[m.slot % 2][:, :].rearrange("p (g d) -> p g d", g=G),
                                         ACT.Copy).then_inc(e_msg, 1)
                z = s.back(3)
                if z.exists(EB):
                    act.wait_ge(e_z, z.n + 1)
                    if z.back(2).exists(EB):
                        act.wait_ge(e_m, z.back(2).n + 1)
                    nc.scalar.activation(tT[:, z.slot % 2, :], ps_z[z.slot % 2][:, :], ACT.Relu, bias=b1_col[:, 0:1])\
                      .then_inc(e_t, 1)

            run_blocks(act, EB, 4, edge_step)
            act.wait_ge(e_rstd, EB)

            def node_step(s):
                if s.exists(NB):
                    act.wait_ge(s_x[s.slot], (s.turn + 1) * 16)
                    if s.back(2).exists(NB):
                        act.wait_ge(n_tr, s.back(2).n + 1)
                    else:
                        act.wait_ge(e_tr, EB)
                    row = s.turn * (U // 2 * T) + s.slot // 2 * T + G + s.slot % 2 * G
                    for g in range(G):
                        last = normalise(xn[:, s.slot % 2, g, :], xb[:, s.slot, g, :], rstd[:, bass.ds(row + g, 1)],
                                         shift[:, bass.ds(row + g, 1)])
                    last.then_inc(n_norm, 1)
                h = s.back(1)
                if h.exists(NB):
                    act.wait_ge(n_tr, h.n + 1)
                    if h.back(2).exists(NB):
                        act.wait_ge(n_u, h.back(2).n + 1)
                    else:
                        act.wait_ge(e_z, EB)
                    nc.scalar.activation(hT[:, h.slot % 2, :], ps_t[h.slot % 2][:, :], ACT.Relu).then_inc(n_h, 1)
                u = s.back(2)
                if u.exists(NB):
                    act.wait_ge(n_u, u.n + 1)
                    if u.back(H).exists(NB):
                        for y_ready in n_y:
                            act.wait_ge(y_ready, u.back(H).n + 1)
                    nc.scalar.activation(r[:, u.slot % H, :, :].rearrange("p g d -> p (g d)"), ps_m[u.slot % 2][:, :],
                                         ACT.Relu).then_inc(n_r, 1)
                f = s.back(3)
                if f.exists(NB):
                    act.wait_ge(n_mom2, f.n + 1)
                    if f.back(R).exists(NB):
                        act.wait_ge(n_rstd2, f.back(R).n + 1)
                    standard_deviation(std2[:, f.slot % R, :], moments2[:, f.slot % R, :, 1]).then_inc(n_std2, 1)
                o = s.back(4)
                if o.exists(NB):
                    act.wait_ge(n_fac2, o.n + 1)
                    for g in range(DVE_TILES, G):
                        last = normalise(r[:, o.slot % H, g, :], r[:, o.slot % H, g, :], rstd2[:, o.slot % R, g:g + 1],
                                         shift2[:, o.slot % R, g:g + 1])
                    last.then_inc(n_ln[1], 1)

            run_blocks(act, NB, 4, node_step)

        @block.vector
        def _(dve):
            chain = [0]

            def link(ins):
                chain[0] += 1
                ins.then_inc(s_set, 1)
                dve.wait_ge(s_set, chain[0])

            def three_parts(parts, bias):
                link(nc.vector.tensor_copy(bias_hi[:, :], bias[:, :]))
                nc.vector.tensor_copy(parts[0:32, :], bias_hi[0:32, :])
                link(nc.vector.tensor_tensor(bias[:, :], bias[:, :], bias_hi[:, :], ALU.subtract))
                link(nc.vector.tensor_copy(bias_hi[:, :], bias[:, :]))
                nc.vector.tensor_copy(parts[32:64, :], bias_hi[32:64, :])
                link(nc.vector.tensor_tensor(bias[:, :], bias[:, :], bias_hi[:, :], ALU.subtract))
                nc.vector.tensor_copy(parts[64:96, :], bias[64:96, :])
                link(nc.vector.tensor_copy(parts[96:128, :], bias[96:128, :]))

            nc.vector.memset(msg[:, :, :, DST:], 0.0)
            nc.vector.memset(table[:, :, 0:2], 0)
            link(nc.vector.memset(ones[:, :], 1.0))
            dve.wait_ge(s_types, 16)
            for k in range(TYPES):
                last = nc.vector.tensor_scalar(type_hot[:, k, :], type_sb[:, :], float(k), None, ALU.is_equal)
            last.then_inc(s_thot, 1)
            dve.wait_ge(s_lists, 32)
            nc.vector.tensor_scalar(q_int[:, 0, :], dst_sb[:, :], PAIR_BITS + QL_BITS, None, ALU.arith_shift_right)
            nc.vector.tensor_scalar(q_int[:, 1, :], dst_sb[:, :], PAIR_BITS, QL - 1, ALU.arith_shift_right,
                                    ALU.bitwise_and)
            nc.vector.tensor_copy(dst_f[:, :], dst_sb[:, :])
            link(nc.vector.tensor_copy(next_f[:, :], next_sb[:, :]))
            nc.vector.tensor_copy(q_f[:, :, :], q_int[:, :, :])
            link(nc.vector.tensor_tensor(next_f[:, :], next_f[:, :], dst_f[:, :], ALU.is_lt))
            nc.vector.tensor_reduce(falls[:, 0:1], next_f[:, :], axis=AX.X, op=ALU.add)
            nc.vector.tensor_reduce(falls[:, 1:2], next_f[:, :], axis=AX.X, op=ALU.add).then_inc(s_falls, 1)
            dve.wait_ge(s_ttr, 1)
            for k in range(TYPES):
                last = nc.vector.tensor_copy(type_turned[:, k, :], ps_z[k][0:SEG, :])
            last.then_inc(s_tcp, 1)
            dve.wait_ge(s_w, 160)
            dve.wait_ge(s_cst, 16)
            nc.vector.tensor_copy(pick_rows[:, :], cst[:, C_ROWS:C_ROWS + P])
            three_parts(b2_parts, b2_bc)
            dve.sem_inc(s_bias, 1)

            def count_pairs():
                dve.wait_ge(e_hist, EB)
                nc.vector.tensor_tensor(counts[:, :], ps_h[:, :], cst[0:G * QH, C_DIAG:C_DIAG + G * QL], ALU.mult)\
                  .then_inc(s_folded, 1)
                dve.wait_ge(s_hist, 2)
                nc.vector.tensor_reduce(count[:, :], ps_q[:, 0:G * QL].rearrange("a (t b) -> a b t", t=G), axis=AX.X,
                                        op=ALU.add)
                link(nc.vector.tensor_scalar(is_sorted[:, :], ps_q[:, G * QL:G * QL + 2], 1.0, None, ALU.is_equal))
                link(nc.vector.tensor_tensor_scan(upto[:, :], ones[0:QH, 0:QL], count[:, :], 0.0, ALU.mult, ALU.add))
                nc.vector.tensor_copy(total[:, :], upto[:, QL - 1:QL].to_broadcast([QH, 2])).then_inc(s_tot, 1)

            def edge_step(s):
                if s.exists(EB):
                    for i in range(2):
                        slot = (2 * s.slot + i) % U
                        dve.wait_ge(s_xa[slot], (s.turn * 2 + ((2 * s.slot + i) // U + 1)) * 16)
                        for g in range(G):
                            nc.vector.bn_stats(stats[:, s.slot % 2, (i + 1) * G + g, :], xb[:, slot, g, :])
                n = s.back(1)
                if n.exists(EB):
                    dve.wait_ge(e_std, n.n + 1)
                    nc.vector.reciprocal(rstd[:, bass.ds(n.n * T, T)], std[:, n.slot % R, :]).then_inc(e_inv, 1)
                if s.exists(EB):
                    if s.back(R).exists(EB):
                        dve.wait_ge(e_hist, s.back(R).n + 1)
                    for hot, i, n_ in ((hot_h, 0, QH), (hot_l, 1, QL)):
                        last = nc.vector.tensor_tensor(
                            hot[:, s.slot % R, :, :], q_f[:, i, bass.ds(s.n * G, G)].unsqueeze(2).to_broadcast([P, G, n_]),
                            cst[:, C_QL:C_QL + n_].unsqueeze(1).to_broadcast([P, G, n_]), ALU.is_equal)
                    last.then_inc(e_hot, 1)
                if n.exists(EB):
                    dve.wait_ge(e_inv, n.n + 1)
                    nc.vector.scalar_tensor_tensor(shift[:, bass.ds(n.n * T, T)], mean_sum[:, n.slot % 2, :], -0.5,
                                                   rstd[:, bass.ds(n.n * T, T)], ALU.mult, ALU.mult).then_inc(e_rstd, 1)
                if s.is_block(EB + 1):
                    count_pairs()
                m = s.back(4)
                if m.exists(EB):
                    if m.back(R).exists(EB):
                        dve.wait_ge(s_mst[m.slot % R], m.use(R) * 16)
                    nc.vector.tensor_copy(msg[:, m.slot % R, :, DST], dst_f[:, bass.ds(m.n * G, G)]).then_inc(e_dst, 1)
                if s.exists(EB):
                    dve.wait_ge(s_gather[s.slot % H], (s.use(H) + 1) * (16 * G))
                    for g in range(G):
                        last = nc.vector.bn_stats(stats[:, s.slot % 2, g, :], xg[:, s.slot % H, g, :])
                    last.then_inc(e_stats, 1)
                    even, odd = stats[:, s.slot % 2, :, 0:3], stats[:, s.slot % 2, :, 3:6]
                    dve.wait_ge(e_stats, s.n + 1)
                    nc.vector.tensor_tensor(mean_gap[:, s.slot % 2, :], even[:, :, 1], odd[:, :, 1], ALU.subtract)
                    nc.vector.tensor_tensor(mean_sum[:, s.slot % 2, :], even[:, :, 1], odd[:, :, 1], ALU.add)
                    nc.vector.tensor_tensor(spread[:, s.slot % 2, :], even[:, :, 2], odd[:, :, 2], ALU.add)\
                      .then_inc(e_sums, 1)
                    dve.wait_ge(e_sums, s.n + 1)
                    nc.vector.scalar_tensor_tensor(mean_gap[:, s.slot % 2, :], mean_gap[:, s.slot % 2, :], D / 4.0,
                                                   mean_gap[:, s.slot % 2, :], ALU.mult, ALU.mult).then_inc(e_gap, 1)
                    dve.wait_ge(e_gap, s.n + 1)
                    nc.vector.tensor_tensor(spread[:, s.slot % 2, :], spread[:, s.slot % 2, :], mean_gap[:, s.slot % 2, :],
                                            ALU.add).then_inc(e_mom, 1)

            run_blocks(dve, EB, 4, edge_step)

            dve.wait_ge(s_off, 1)
            link(nc.vector.tensor_copy(offset[:, :], ps_q[:, G * QL + 2:G * QL + 4]))
            link(nc.vector.tensor_tensor(upto[:, :], upto[:, :], count[:, :], ALU.subtract))
            nc.vector.tensor_scalar(tab_f[:, 0, :], upto[:, :], offset[:, 0:1], is_sorted[:, 0:1], ALU.add, ALU.mult)
            link(nc.vector.tensor_scalar(total[:, :], is_sorted[:, :], 1.0 - EP, float(EP), ALU.mult, ALU.add))
            link(nc.vector.tensor_scalar(tab_f[:, 1, :], count[:, :], total[:, 0:1], -1.0, ALU.max, ALU.add))
            link(nc.vector.tensor_copy(tab_i[:, :, :], tab_f[:, :, :]))
            nc.vector.tensor_scalar(tab_i[:, 1, :], tab_i[:, 1, :], WINDOW_BITS, None, ALU.arith_shift_right)\
              .then_inc(s_tabi, 1)

            three_parts(bs_parts, bs_bc)
            dve.sem_inc(s_bs, 1)

            dve.wait_ge(s_tab, 32)
            turns = running_counts(dve, "dve")
            read_table = table_reader(dve, 1, (1,))

            def select_extra(s, q, to, window):
                return nc.vector.tensor_scalar(to, slot_of, window[:, DST:DST + 1],
                                               cst[:, bass.ds(s.n * 2 + C_BASE + q, 1)], ALU.subtract, ALU.is_equal)

            def node_step(s):
                f = s.back(3)
                if f.exists(NB):
                    dve.wait_ge(n_r, f.n + 1)
                    for g in range(G):
                        last = nc.vector.bn_stats(stats2[:, f.slot % 2, g, :], r[:, f.slot % H, g, :])
                    last.then_inc(n_stats2, 1)
                o = s.back(4)
                if o.exists(NB):
                    dve.wait_ge(n_std2, o.n + 1)
                    if o.back(R).exists(NB):
                        dve.wait_ge(n_gam, o.back(R).n + 1)
                    nc.vector.reciprocal(rstd2[:, o.slot % R, :], std2[:, o.slot % R, :]).then_inc(n_rstd2, 1)
                w = s.back(1)
                if w.exists(NB):
                    dve.wait_ge(n_rel, w.n + 1)
                    if w.back(2).exists(NB):
                        dve.wait_ge(n_u, w.back(2).n + 1)
                    for q in range(2):
                        last = nc.vector.tensor_scalar(sel[:, w.slot % 2, q, :], slot_of, rel[:, w.slot % R, q:q + 1],
                                                       None, ALU.is_equal)
                    last.then_inc(n_sel, 1)
                if o.exists(NB):
                    dve.wait_ge(n_rstd2, o.n + 1)
                    nc.vector.scalar_tensor_tensor(shift2[:, o.slot % R, :], moments2[:, o.slot % R, :, 0], -1.0,
                                                   rstd2[:, o.slot % R, :], ALU.mult, ALU.mult).then_inc(n_fac2, 1)
                elif f.exists(NB):
                    wait_ahead(dve, n_stats2, f.n + 1)
                if f.exists(NB):
                    for g in range(G):
                        last = nc.vector.bn_aggr(moments2[:, f.slot % R, g, :], stats2[:, f.slot % 2, g, :])
                    last.then_inc(n_mom2, 1)
                if o.exists(NB):
                    dve.wait_ge(n_fac2, o.n + 1)
                    for g in range(DVE_TILES):
                        last = nc.vector.tensor_scalar(r[:, o.slot % H, g, :], r[:, o.slot % H, g, :],
                                                       rstd2[:, o.slot % R, g:g + 1], shift2[:, o.slot % R, g:g + 1],
                                                       ALU.mult, ALU.add)
                    last.then_inc(n_ln[0], 1)
                counts, = read_table(s)
                y_ = s.back(6)
                if y_.exists(NB):
                    dve.wait_ge(n_gam, y_.n + 1)
                    dve.wait_ge(n_xb, y_.n + 1)
                    if y_.back(R).exists(NB):
                        dve.wait_ge(s_out[y_.slot % R], y_.use(R) * 16)
                    nc.vector.tensor_tensor(y[:, y_.slot % R, 0:Y_TILES, :], r[:, y_.slot % H, 0:Y_TILES, :],
                                            xb[:, y_.slot, 0:Y_TILES, :], ALU.add).then_inc(n_y[0], 1)
                if w.exists(NB):
                    def select_second(es):
                        for q in range(2):
                            last = select_extra(w, q, sel_x[:, es, q, :], win[:, w.slot % R, q, 1, :])
                        last.then_inc(x_sel[es], 1)

                    def select_later(q, es, c):
                        done = dve.snap(turns[es])
                        dve.wait_ge(s_winx[es], (done + 1) * 16)
                        dve.wait_ge(x_used[es], done + 1)
                        for i in range(2):
                            last = select_extra(w, q, sel_x[:, es, i, :], win_x[:, es, i, :])
                        last.then_inc(x_sel[es], 1)

                    for_extras(dve, w, counts, turns, select_second, select_later)

            run_blocks(dve, NB, 6, node_step)

        @block.tensor
        def _(pe):
            pe.wait_ge(s_cst, 16)
            pe.wait_ge(s_thot, 1)
            for k in range(TYPES):
                for c in range(G):
                    last = nc.tensor.transpose(ps_z[k][0:SEG, c * P:(c + 1) * P], type_hot[:, k, c * SEG:(c + 1) * SEG],
                                               ident)
            last.then_inc(s_ttr, 1)
            pe.wait_ge(s_falls, 1)
            nc.tensor.matmul(ps_q[:, G * QL:G * QL + 2], ones[:, 0:QH], falls[:, :], start=True, stop=True)\
              .then_inc(s_hist, 1)
            pe.wait_ge(s_w, 160)
            pe.wait_ge(s_bias, 1)

            def edge_step(s):
                if s.is_block(EB):
                    pe.wait_ge(s_folded, 1)
                    nc.tensor.matmul(ps_q[:, 0:G * QL], cst[0:G * QH, C_FOLD:C_FOLD + QH], counts[:, :], start=True,
                                     stop=True).then_inc(s_hist, 1)
                if s.is_block(EB + 1):
                    pe.wait_ge(s_tot, 1)
                    nc.tensor.matmul(ps_q[:, G * QL + 2:G * QL + 4], tri[0:QH, 0:QH], total[:, :], start=True, stop=True)\
                      .then_inc(s_off, 1)
                if s.exists(EB):
                    pe.wait_ge(e_hot, s.n + 1)
                    nc.tensor.matmul(ps_h[:, :], hot_h[:, s.slot % R, :, :].rearrange("p t a -> p (t a)"),
                                     hot_l[:, s.slot % R, :, :].rearrange("p t a -> p (t a)"),
                                     start=s.is_block(0), stop=s.is_block(EB - 1)).then_inc(e_hist, 1)
                if s.exists(EB):
                    pe.wait_ge(e_norm, s.n + 1)
                    if s.back(2).exists(EB):
                        pe.wait_ge(e_h, s.back(2).n + 1)
                    for g in range(G):
                        last = nc.tensor.transpose(ps_t[s.slot % 2][:, g * P:(g + 1) * P], xn[:, s.slot % 2, g, :], ident)
                    last.then_inc(e_tr, 1)
                z = s.back(1)
                if z.exists(EB):
                    pe.wait_ge(s_ez[z.slot % H], (z.use(H) + 1) * 32)
                    if z.back(2).exists(EB):
                        pe.wait_ge(e_t, z.back(2).n + 1)
                    nc.tensor.matmul(ps_z[z.slot % 2][:, :], w1_e[:, :], ez[:, z.slot % H, :], start=True, stop=False)
                    pe.wait_ge(e_h, z.n + 1)
                    nc.tensor.matmul(ps_z[z.slot % 2][:, :], w1_x[:, :], hT[:, z.slot % 2, :], start=False, stop=True)\
                      .then_inc(e_z, 1)
                m = s.back(2)
                if m.exists(EB):
                    if m.back(2).exists(EB):
                        pe.wait_ge(e_msg, m.back(2).n + 1)
                    nc.tensor.matmul(ps_m[m.slot % 2][:, :], pick_rows[:, :], b2_parts[:, :], start=True, stop=False)
                    pe.wait_ge(e_t, m.n + 1)
                    for g in range(G):
                        last = nc.tensor.matmul(ps_m[m.slot % 2][:, g * D:(g + 1) * D],
                                                tT[:, m.slot % 2, g * P:(g + 1) * P], w2_sb[:, :], start=False,
                                                stop=(g == G - 1))
                    last.then_inc(e_m, 1)

            run_blocks(pe, EB, 2, edge_step)

            pe.wait_ge(s_bs, 1)
            turns = running_counts(pe, "pe")
            read_table = table_reader(pe, 1, (1,))
            for i in range(LATER):
                pe.sem_inc(x_used[i], 1)

            def node_step(s):
                if s.exists(NB):
                    pe.wait_ge(n_norm, s.n + 1)
                    if s.back(2).exists(NB):
                        pe.wait_ge(n_h, s.back(2).n + 1)
                    else:
                        pe.wait_ge(e_h, EB)
                    for g in range(G):
                        last = nc.tensor.transpose(ps_t[s.slot % 2][:, g * P:(g + 1) * P], xn[:, s.slot % 2, g, :], ident)
                    last.then_inc(n_tr, 1)
                if s.is_block(0):
                    pe.wait_ge(s_tab, 32)
                counts, = read_table(s)
                u = s.back(1)
                if u.exists(NB):
                    ps_u = ps_m[u.slot % 2]
                    if u.back(2).exists(NB):
                        pe.wait_ge(n_r, u.back(2).n + 1)
                    else:
                        pe.wait_ge(e_msg, EB)
                    nc.tensor.matmul(ps_u[:, :], pick_rows[:, :], bs_parts[:, :], start=True, stop=False)
                    pe.wait_ge(n_h, u.n + 1)
                    for g in range(G):
                        nc.tensor.matmul(ps_u[:, g * D:(g + 1) * D], hT[:, u.slot % 2, g * P:(g + 1) * P], ws_sb[:, :],
                                         start=False, stop=False)
                    def multiply(es, pairs, windows):
                        pe.wait_ge(x_sel[es], pe.snap(turns[es]) + 1)
                        for i in range(2):
                            for k in range(2):
                                g = 2 * pairs[i] + k
                                last = nc.tensor.matmul(ps_u[:, g * D:(g + 1) * D], sel_x[:, es, i, k * P:(k + 1) * P],
                                                        windows[i][:, 0:D], start=False, stop=False)
                        return last

                    for_extras(pe, u, counts, turns,
                               lambda es: multiply(es, (0, 1), [win[:, u.slot % R, q, 1, :] for q in range(2)]),
                               lambda q, es, c: multiply(es, (q, q), [win_x[:, es, i, :] for i in range(2)])
                               .then_inc(x_used[es], 1))
                    pe.wait_ge(n_sel, u.n + 1)
                    for q in range(2):
                        for k in range(2):
                            g = 2 * q + k
                            last = nc.tensor.matmul(ps_u[:, g * D:(g + 1) * D], sel[:, u.slot % 2, q, k * P:(k + 1) * P],
                                                    win[:, u.slot % R, q, 0, 0:D], start=False, stop=(g == G - 1))
                    last.then_inc(n_u, 1)

            run_blocks(pe, NB, 1, node_step)


def kernel(x, src, dst, edge_attr_16, edge_type_2, L0_gnn_W1, L0_gnn_b1, L0_gnn_W2, L0_gnn_b2, L0_gnn_Ws, L0_gnn_bs,
           L0_gnn_gamma, L0_gnn_beta):
    import concourse.bacc as bacc
    from concourse.bass_utils import run_bass_kernel_spmd

    def padded(a, rows, fill=0):
        a = np.asarray(a)
        whole = np.full((rows,) + a.shape[1:], fill, a.dtype)
        whole[:len(a)] = a
        return whole

    dst_all = padded(dst, EP + 1, -1)
    feats = padded(edge_attr_16, EP).reshape(P, EB, G, EF).transpose(1, 3, 2, 0).reshape(EB, EF, BLK)

    consts = np.zeros((P, C_END), np.float32)
    consts[:, C_ID:C_ID + P] = np.eye(P)
    consts[:, C_SLOT:C_SLOT + PAIR] = np.arange(PAIR).reshape(P, 2).T.reshape(1, PAIR)
    consts[:, C_BASE:C_BASE + PAIRS] = -np.arange(0, NP, PAIR)
    consts[:, C_QL:C_QL + QL] = np.arange(QL)
    consts[:, C_TRI:C_TRI + P] = np.triu(np.ones((P, P)), 1)
    consts[[0, 32, 64], C_ROWS:C_ROWS + P] = 1.0
    consts[:, C_EPS] = EPS
    consts[:G * QH, C_DIAG:C_DIAG + G * QL] = np.kron(np.eye(G), np.ones((QH, QL)))
    consts[:G * QH, C_FOLD:C_FOLD + QH] = np.tile(np.eye(QH), (G, 1))

    arrays = {
        "x": padded(x, NP), "src": padded(src, EP).reshape(P, ET), "dst": dst_all[:EP].reshape(P, ET),
        "dst_next": dst_all[1:].reshape(P, ET), "types": padded(edge_type_2, EP).reshape(P, ET), "feats": feats,
        "w1": L0_gnn_W1, "b1": np.asarray(L0_gnn_b1).reshape(D, 1), "w2": L0_gnn_W2, "b2": np.tile(np.asarray(L0_gnn_b2), G), "ws": L0_gnn_Ws,
        "bs": np.tile(np.asarray(L0_gnn_bs), G), "gamma": L0_gnn_gamma, "beta": L0_gnn_beta, "consts": consts,
    }
    arrays = {f"in_{k}": np.ascontiguousarray(a) for k, a in arrays.items()}
    nc = bacc.Bacc("TRN2", target_bir_lowering=False, num_devices=1)
    args = [nc.dram_tensor(k, a.shape, mybir.dt.from_np(a.dtype), kind="ExternalInput").ap() for k, a in arrays.items()]
    out = nc.dram_tensor("out", (NP, D), mybir.dt.float32, kind="ExternalOutput").ap()
    build(nc, *args, out)
    result = run_bass_kernel_spmd(nc, [arrays], core_ids=[0])
    return result.results[0]["out"][:N]
```
